# Optimizing a Trainium2 kernel written in Bass

```python
import numpy as np
import jax
import jax.numpy as jnp

def _softmax(x, axis=-1):
    return jax.nn.softmax(x, axis=axis)

def _gelu(x):
    return jax.nn.gelu(x, approximate=True)

def _silu(x):
    return jax.nn.silu(x)

def _sigmoid(x):
    return jax.nn.sigmoid(x)

def _layernorm(x, axis=-1, eps=1e-05):
    m = jnp.mean(x, axis=axis, keepdims=True)
    v = jnp.var(x, axis=axis, keepdims=True)
    return (x - m) / jnp.sqrt(v + eps)

def _scatter_add(tgt, idx, src, axis=0):
    return tgt.at[idx].add(src)

def _segment_sum(src, seg, n):
    return jax.ops.segment_sum(src, seg, n)
kernel_name = 'mk_audio_tower_d1_tok_audfeat256_r4_52a041'

def setup_inputs(seed: int=0):
    np.random.seed(seed)
    _w = jnp.asarray

    def _rec_inputs():
        import jax
        import jax.numpy as jnp
        _rk = jax.random.key(seed)
        x = 1.50771e-05 + 1.00003 * jax.random.normal(jax.random.fold_in(_rk, 1), (32, 256, 64), jnp.float32)
        return x
    x = _rec_inputs()

    def _L0_tok_setup():
        import jax, jax.numpy as jnp
        from jax import lax
        import numpy as np
        POOL_SIZE = 2

        def _max_pool_same(x, window, stride):
            W = x.shape[1]
            out = -(-W // stride)
            pad_total = max((out - 1) * stride + window - W, 0)
            pad_lo = pad_total // 2
            pad_hi = pad_total - pad_lo
            return lax.reduce_window(x, -jnp.inf, lax.max, window_dimensions=(1, window, 1), window_strides=(1, stride, 1), padding=[(0, 0), (pad_lo, pad_hi), (0, 0)])
        key = jax.random.key(seed)
        B, W, C = (16, 4096, 64)
        x = jax.random.normal(key, (B, W, C), dtype=jnp.float32)
        blur_kernel = jnp.array([2.0, 4.0, 2.0], dtype=jnp.float32) / 8.0
        return {'x': x, 'blur_kernel': blur_kernel}
    _L0_tok_all = _L0_tok_setup()
    _L0_tok_in = {k: v for k, v in _L0_tok_all.items() if k in ('blur_kernel',)}
    del _L0_tok_all

    def _L0_attn_setup():
        import jax, jax.numpy as jnp
        import numpy as np
        NEG_INF = 1e+32
        key = jax.random.key(seed)
        ks = jax.random.split(key, 7)
        B, S, C, DK, DO = (16, 512, 64, 64, 64)
        sc = 1.0 / np.sqrt(C)
        return {'x': jax.random.normal(ks[0], (B, S, C), jnp.float32), 'Wq': jax.random.normal(ks[1], (C, DK), jnp.float32) * sc, 'bq': jnp.zeros((DK,), jnp.float32), 'Wk': jax.random.normal(ks[2], (C, DK), jnp.float32) * sc, 'bk': jnp.zeros((DK,), jnp.float32), 'Wv': jax.random.normal(ks[3], (C, DO), jnp.float32) * sc, 'bv': jnp.zeros((DO,), jnp.float32)}
    _L0_attn_all = _L0_attn_setup()
    _L0_attn_in = {k: v for k, v in _L0_attn_all.items() if k in ('Wq', 'bq', 'Wk', 'bk', 'Wv', 'bv')}
    del _L0_attn_all

    def _L0_ffn_setup():
        import jax, jax.numpy as jnp
        import numpy as np
        E = 8
        K = 2
        D = 64
        H = 128
        DOUT = 64
        EPS = 1e-05
        key = jax.random.key(seed)
        ks = jax.random.split(key, 9)
        s = 0.02
        return {'x': jax.random.normal(ks[0], (4, 2048, D), jnp.float32), 'gamma': 1.0 + 0.05 * jax.random.normal(ks[1], (D,), jnp.float32), 'beta': 0.05 * jax.random.normal(ks[2], (D,), jnp.float32), 'Wr': 0.01 * jax.random.normal(ks[3], (D, E), jnp.float32), 'br': jnp.zeros((E,), jnp.float32), 'W1': s * jax.random.normal(ks[4], (E, D, H), jnp.float32), 'b1': s * jax.random.normal(ks[5], (E, H), jnp.float32), 'W2': s * jax.random.normal(ks[6], (E, H, DOUT), jnp.float32), 'b2': s * jax.random.normal(ks[7], (E, DOUT), jnp.float32)}
    _L0_ffn_all = _L0_ffn_setup()
    _L0_ffn_in = {k: v for k, v in _L0_ffn_all.items() if k in ('gamma', 'beta', 'Wr', 'br', 'W1', 'b1', 'W2', 'b2')}
    del _L0_ffn_all
    return {'x': x, 'L0_tok_blur_kernel': _L0_tok_in['blur_kernel'], 'L0_attn_Wq': _L0_attn_in['Wq'], 'L0_attn_bq': _L0_attn_in['bq'], 'L0_attn_Wk': _L0_attn_in['Wk'], 'L0_attn_bk': _L0_attn_in['bk'], 'L0_attn_Wv': _L0_attn_in['Wv'], 'L0_attn_bv': _L0_attn_in['bv'], 'L0_ffn_gamma': _L0_ffn_in['gamma'], 'L0_ffn_beta': _L0_ffn_in['beta'], 'L0_ffn_Wr': _L0_ffn_in['Wr'], 'L0_ffn_br': _L0_ffn_in['br'], 'L0_ffn_W1': _L0_ffn_in['W1'], 'L0_ffn_b1': _L0_ffn_in['b1'], 'L0_ffn_W2': _L0_ffn_in['W2'], 'L0_ffn_b2': _L0_ffn_in['b2']}

def reference(x, L0_tok_blur_kernel, L0_attn_Wq, L0_attn_bq, L0_attn_Wk, L0_attn_bk, L0_attn_Wv, L0_attn_bv, L0_ffn_gamma, L0_ffn_beta, L0_ffn_Wr, L0_ffn_br, L0_ffn_W1, L0_ffn_b1, L0_ffn_W2, L0_ffn_b2):
    import jax
    import jax.numpy as jnp

    def _L0_tok_ref(x, blur_kernel):
        import jax, jax.numpy as jnp
        from jax import lax
        import numpy as np
        POOL_SIZE = 2

        def _max_pool_same(x, window, stride):
            W = x.shape[1]
            out = -(-W // stride)
            pad_total = max((out - 1) * stride + window - W, 0)
            pad_lo = pad_total // 2
            pad_hi = pad_total - pad_lo
            return lax.reduce_window(x, -jnp.inf, lax.max, window_dimensions=(1, window, 1), window_strides=(1, stride, 1), padding=[(0, 0), (pad_lo, pad_hi), (0, 0)])
        C = x.shape[2]
        x = _max_pool_same(x, POOL_SIZE, 1)
        w = jnp.broadcast_to(blur_kernel.reshape(3, 1, 1), (3, 1, C))
        x = lax.conv_general_dilated(x, w, window_strides=(1,), padding='SAME', dimension_numbers=('NWC', 'WIO', 'NWC'), feature_group_count=C)
        x = _max_pool_same(x, POOL_SIZE, POOL_SIZE)
        return x

    def _L0_attn_ref(x, Wq, bq, Wk, bk, Wv, bv):
        import jax, jax.numpy as jnp
        import numpy as np
        NEG_INF = 1e+32
        dk = Wq.shape[-1]
        Q = x @ Wq + bq
        K = x @ Wk + bk
        V = x @ Wv + bv
        attn = jnp.einsum('bqd,bkd->bqk', Q, K) / jnp.sqrt(jnp.float32(dk))
        S = attn.shape[1]
        causal = jnp.tril(jnp.ones((S, S), jnp.float32))
        attn = causal * attn + (1.0 - causal) * -NEG_INF
        probs = jax.nn.softmax(attn, axis=2)
        return jnp.einsum('bqk,bkd->bqd', probs, V)

    def _L0_ffn_ref(x, gamma, beta, Wr, br, W1, b1, W2, b2):
        import jax, jax.numpy as jnp
        import numpy as np
        E = 8
        K = 2
        D = 64
        H = 128
        DOUT = 64
        EPS = 1e-05
        mu = jnp.mean(x, axis=-1, keepdims=True)
        var = jnp.mean(jnp.square(x - mu), axis=-1, keepdims=True)
        xn = (x - mu) * jax.lax.rsqrt(var + EPS) * gamma + beta
        logits = jnp.einsum('bsd,de->bse', xn, Wr) + br
        top_vals, top_idx = jax.lax.top_k(logits, K)
        w = jax.nn.softmax(top_vals, axis=-1)
        w_full = jnp.einsum('bsk,bske->bse', w, jax.nn.one_hot(top_idx, E, dtype=w.dtype))
        y = jnp.zeros(x.shape[:-1] + (DOUT,), x.dtype)
        for e in range(E):
            h = jax.nn.gelu(jnp.einsum('bsd,dh->bsh', xn, W1[e]) + b1[e], approximate=False)
            y_e = jnp.einsum('bsh,hd->bsd', h, W2[e]) + b2[e]
            y = y + y_e * w_full[..., e, None]
        return y
    h = _L0_tok_ref(x, L0_tok_blur_kernel)
    h = h + _L0_attn_ref(_layernorm(h, axis=-1), L0_attn_Wq, L0_attn_bq, L0_attn_Wk, L0_attn_bk, L0_attn_Wv, L0_attn_bv)
    h = h + _L0_ffn_ref(_layernorm(h, axis=-1), L0_ffn_gamma, L0_ffn_beta, L0_ffn_Wr, L0_ffn_br, L0_ffn_W1, L0_ffn_b1, L0_ffn_W2, L0_ffn_b2)
    return h

_drawn_inputs = setup_inputs


def setup_inputs(seed=0):
    import zlib

    import numpy as np

    out = dict(_drawn_inputs(seed))
    spreads = {'L0_attn_bq': (0.0, 0.407),
     'L0_attn_bk': (0.0, 2.0),
     'L0_attn_bv': (0.0, 0.1),
     'L0_ffn_br': (0.0, 0.365)}
    factors = {'L0_ffn_gamma': 8.0,
     'L0_ffn_beta': 8.0,
     'L0_ffn_Wr': 6.535,
     'L0_ffn_W1': 4.413,
     'L0_ffn_b1': 8.0,
     'L0_ffn_W2': 4.405,
     'L0_ffn_b2': 11.952}
    for name, (base, spread) in spreads.items():
        noise = np.random.default_rng([zlib.crc32(name.encode()), seed]).standard_normal(out[name].shape)
        drawn = base * np.exp(spread * noise) if base else spread * noise
        out[name] = jnp.asarray(drawn.astype(out[name].dtype))
    for name, factor in factors.items():
        out[name] = (out[name] * factor).astype(out[name].dtype)
    return out
```

```python
from contextlib import ExitStack

import concourse.bass as bass
from concourse import mybir

ALU = mybir.AluOpType
ACT = mybir.ActivationFunctionType
AX = mybir.AxisListType
F32 = mybir.dt.float32
F32R = mybir.dt.float32r
BF16 = mybir.dt.bfloat16
U32 = mybir.dt.uint32

P = 128
STAGES = 5
SMOOTH, PROJECT, ATTEND, EXPERTS, CLOSE = range(STAGES)


class Tile:

    def __init__(self, i, offset):
        self.i, self.offset = i, offset
        self.parity = offset % 2
        self.n = 2 * i + offset
        self.fixed = isinstance(i, int)

    def has_before(self, back):
        return not self.fixed or self.n >= back

    def count(self, per=1, k=None, back=0):
        return per * (self.n - back) + (per if k is None else k)

    def turns(self, per, back=0):
        return per * (self.i + (self.offset - back) // 2 + 1)


def pipeline(engine, tiles, step):

    def fixed(k):
        return [Tile(0, k - s) if 0 <= k - s < tiles else None for s in range(STAGES)]

    first = STAGES - 1
    full = tiles - first
    assert full % 2 == 0 and first % 2 == 0
    for k in range(first):
        step(fixed(k))
    with engine.Fori(0, full // 2) as i:
        for odd in range(2):
            step([Tile(i, first + odd - s) for s in range(STAGES)])
    for k in range(tiles, tiles + first):
        step(fixed(k))


def audio_tower(nc, x, taps, wq, bq, wk, bk, wv, bv, gamma, beta, wr, br, w1, b1, w2, b2, out, w_dram):
    BATCH, TIME, C = x.shape
    T = TIME // 2
    E, _, H = w1.shape
    J = 4
    TILES = BATCH // J
    N = J * T
    PAIRS = E // 2
    DK = wq.shape[1]
    SCALE = float(DK) ** -0.5
    EPS = 1e-5
    MASKED = -1e32
    LOWEST = -3.0e38
    FIRST = STAGES - 1
    assert T == P and 2 * C == P and H == P and N == 512 and DK == C and E == 8

    with ExitStack() as ctx:
        ctx.enter_context(nc.allow_non_contiguous_dma(reason="biases of a few KiB, loaded once"))

        def sb(name, shape, dt=F32):
            return ctx.enter_context(nc.sbuf_tensor(name, shape, dt))

        def bank(name):
            return ctx.enter_context(nc.psum_tensor(name, [P, 512], F32))

        def sem(name):
            return ctx.enter_context(nc.semaphore(name))

        ident = sb("ident", [P, P])
        ident16 = sb("ident16", [P, P], BF16)
        mask16 = sb("mask16", [P, J, T], BF16)
        two_ident = sb("two_ident", [P, C])
        iota = sb("iota", [P, E])
        minus_half = sb("minus_half", [P, J])

        taps_sb = sb("taps_sb", [P, 3])
        wqk = sb("wqk", [P, 2 * DK])
        wqk_hi = sb("wqk_hi", [P, 2 * DK], F32R)
        wqk_lo = sb("wqk_lo", [P, 2 * DK], F32R)
        bqk = sb("bqk", [P, 1])
        wv_sb = sb("wv_sb", [P, C])
        wv_hl = sb("wv_hl", [P, 2, C], F32R)
        bv_sb = sb("bv_sb", [P, C])
        gamma_sb = sb("gamma_sb", [P, 1])
        beta_sb = sb("beta_sb", [P, 1])
        beta_row = sb("beta_row", [C, P])
        wr_sb = sb("wr_sb", [P, E])
        wr_g = sb("wr_g", [P, E])
        wr_hl = sb("wr_hl", [P, 2, E], F32R)
        br_sb = sb("br_sb", [P, E])
        br_f = sb("br_f", [P, E])
        w1_sb = sb("w1_sb", [P, E, H])
        w1_g = sb("w1_g", [P, E, H])
        w1_hi = sb("w1_hi", [P, E, H], F32R)
        w1_lo = sb("w1_lo", [P, E, H], F32R)
        b1_sb = sb("b1_sb", [P, E])
        b1_f = sb("b1_f", [P, E])
        w2_sb = sb("w2_sb", [P, E, C])
        b2_sb = sb("b2_sb", [P, PAIRS])

        x_sb = sb("x_sb", [P, 3, BATCH, C])
        y_sb = [sb(f"y_sb{i}", [P, 4, J, C]) for i in range(2)]
        z_sb = sb("z_sb", [P, 2, J, C])
        h_sb = [sb(f"h_sb{i}", [P, J, C]) for i in range(2)]
        hb_sb = [sb(f"hb_sb{i}", [P, J, C]) for i in range(2)]
        h2_sb = [sb(f"h2_sb{i}", [P, J, C]) for i in range(2)]
        stats1 = sb("stats1", [P, J, 6])
        mom1 = [sb(f"mom1_{i}", [P, J, 2]) for i in range(2)]
        ve1 = sb("ve1", [P, J])
        rstd1 = [sb(f"rstd1_{i}", [P, J]) for i in range(2)]
        xh1 = sb("xh1", [P, J, C])
        split1 = sb("split1", [P, J, 2, C])
        x1t = sb("x1t", [P, N], F32R)
        qt = sb("qt", [DK, N])
        kt = sb("kt", [DK, N])
        v_part = sb("v_part", [P, J, C])
        v_sb = [sb(f"v_sb{i}", [P, J, C + 1]) for i in range(2)]
        top = [sb(f"top{i}", [P, J]) for i in range(2)]
        probs = sb("probs", [P, J, T])
        probs_t = sb("probs_t", [P, J, T])
        rsum = sb("rsum", [P, J])
        stats2 = sb("stats2", [P, J, 6])
        mom2 = sb("mom2", [P, J, 2])
        ve2 = sb("ve2", [P, J])
        rstd2 = sb("rstd2", [P, J])
        xh2 = sb("xh2", [P, J, C])
        split2 = sb("split2", [P, J, 2, C])
        x2t = [sb(f"x2t{i}", [P, N], F32R) for i in range(2)]
        lg_part = sb("lg_part", [P, J, E])
        lg = sb("lg", [P, J, E])
        best = sb("best", [P, J, 8])
        which = sb("which", [P, J, 8], U32)
        which_f = sb("which_f", [P, J, 2])
        gap = sb("gap", [P, J])
        tanh_gap = sb("tanh_gap", [P, J])
        share = sb("share", [P, 2, J])
        hot = sb("hot", [P, 2, J, E])
        hot_w = sb("hot_w", [P, 2, J, E])
        w_sb = sb("w_sb", [P, E, J])
        w_t = sb("w_t", [E * J, T])
        w_bc = [sb(f"w_bc{i}", [P, PAIRS, N]) for i in range(2)]
        g_sb = [sb(f"g_sb{i}", [P, N]) for i in range(4)]
        yw = [sb(f"yw{i}", [P, N]) for i in range(PAIRS)]
        y01 = sb("y01", [P, N])
        y012 = sb("y012", [P, N])
        y_sum = sb("y_sum", [P, N])
        o_sb = [sb(f"o_sb{i}", [P, J, C]) for i in range(2)]

        turned = bank("turned")
        mixed = bank("mixed")
        values = bank("values")
        small = bank("small")
        hidden = [bank(f"hidden{i}") for i in range(2)]
        expert = [bank(f"expert{i}") for i in range(2)]

        w_in = sem("w_in")
        x_first = [sem(f"x_first{i}") for i in range(FIRST)]
        x_rest = sem("x_rest")
        edges = sem("edges")
        consts = sem("consts")
        folded = sem("folded")
        w_ready = sem("w_ready")
        w_step = sem("w_step")
        y_ready = sem("y_ready")
        y_shifted = [sem(f"y_shifted{i}") for i in range(2)]
        blur_step = sem("blur_step")
        h_ready = sem("h_ready")
        hb_ready = sem("hb_ready")
        stats1_ready = sem("stats1_ready")
        mom1_ready = sem("mom1_ready")
        ve1_ready = sem("ve1_ready")
        rstd1_ready = sem("rstd1_ready")
        xh1_ready = sem("xh1_ready")
        hi1_ready = sem("hi1_ready")
        split1_ready = sem("split1_ready")
        x1_turned = sem("x1_turned")
        x1t_ready = sem("x1t_ready")
        qk_done = sem("qk_done")
        v_done = sem("v_done")
        qk_ready = sem("qk_ready")
        v_part_ready = sem("v_part_ready")
        v_ready = sem("v_ready")
        scores_done = sem("scores_done")
        top_ready = sem("top_ready")
        probs_ready = sem("probs_ready")
        probs_turned = sem("probs_turned")
        probs_t_ready = sem("probs_t_ready")
        attn_done = sem("attn_done")
        rsum_ready = sem("rsum_ready")
        h2_ready = sem("h2_ready")
        stats2_ready = sem("stats2_ready")
        mom2_ready = sem("mom2_ready")
        ve2_ready = sem("ve2_ready")
        rstd2_ready = sem("rstd2_ready")
        xh2_ready = sem("xh2_ready")
        hi2_ready = sem("hi2_ready")
        split2_ready = sem("split2_ready")
        x2_turned = sem("x2_turned")
        x2t_ready = sem("x2t_ready")
        lg_done = sem("lg_done")
        lg_step = sem("lg_step")
        gap_ready = sem("gap_ready")
        tanh_ready = sem("tanh_ready")
        route_step = sem("route_step")
        w_sb_ready = sem("w_sb_ready")
        w_turned = sem("w_turned")
        w_t_ready = sem("w_t_ready")
        w_spilled = [sem(f"w_spilled{i}") for i in range(2)]
        w_spread = [sem(f"w_spread{i}") for i in range(2)]
        hidden_done = sem("hidden_done")
        g_ready = sem("g_ready")
        expert_done = sem("expert_done")
        yw_ready = sem("yw_ready")
        sum_step = sem("sum_step")
        closed = sem("closed")
        o_ready = sem("o_ready")
        stored = [sem(f"stored{i}") for i in range(2)]

        N_WEIGHTS = 20

        block = ctx.enter_context(nc.Block())

        @block.sync
        def _(sp):
            rows = x.rearrange("b (t r) c -> t r b c", r=2)
            for n in range(FIRST + 1):
                lo, hi = (n * J, (n + 1) * J) if n < FIRST else (FIRST * J, BATCH)
                landed = x_first[n] if n < FIRST else x_rest
                if n == 0:
                    sp.wait_ge(edges, 1)
                for r in range(2):
                    sp.dma_start(x_sb[:, r, lo:hi, :], rows[:, r, lo:hi, :]).then_inc(landed, 16)
                for a, b in ((0, 112), (112, T - 1)):
                    sp.dma_start(x_sb[a:b, 2, lo:hi, :], rows[a + 1:b + 1, 0, lo:hi, :]).then_inc(landed, 16)

            def step(stages):
                smooth, project, attend, experts, close = stages
                if smooth:
                    c = smooth
                    y = y_sb[c.parity]
                    sp.wait_ge(y_ready, c.count())
                    for a, b in ((0, 112), (112, T - 1)):
                        sp.dma_start(y[a + 1:b + 1, 0], y[a:b, 2]).then_inc(y_shifted[c.parity], 16)
                        sp.dma_start(y[a:b, 3], y[a + 1:b + 1, 1]).then_inc(y_shifted[c.parity], 16)
                if close:
                    c = close
                    sp.wait_ge(o_ready, c.count())
                    sp.dma_start(
                        out.rearrange("(n j) t c -> n t j c", j=J)[bass.ds(c.n, 1), :, :, :].rearrange("n t j c -> (n t) j c")
                        if not c.fixed else out[c.n * J:(c.n + 1) * J].rearrange("j t c -> t j c"),
                        o_sb[c.parity][:]).then_inc(stored[c.parity], 16)
                if attend:
                    c = attend
                    sp.wait_ge(w_t_ready, c.count())
                    sp.dma_start(w_dram[c.parity].rearrange("(a t) -> a t", t=T), w_t[:]).then_inc(w_spilled[c.parity], 16)
                    sp.wait_ge(w_spilled[c.parity], c.turns(16))
                    if c.has_before(2):
                        sp.wait_ge(yw_ready, c.count(PAIRS, back=2))
                    for half in range(2):
                        sp.dma_start(
                            w_bc[c.parity][half * C:(half + 1) * C],
                            w_dram[c.parity].rearrange("(p h t) -> h p t", h=2, t=N)[half].unsqueeze(0).to_broadcast([C, PAIRS, N]),
                        ).then_inc(w_spread[c.parity], 16)

            pipeline(sp, TILES, step)
            for i in range(2):
                sp.wait_ge(stored[i], 16 * TILES // 2)

        @block.gpsimd
        def _(pool):
            nc.gpsimd.memset(x_sb[:, 2], LOWEST).then_inc(edges, 1)
            for y in y_sb:
                nc.gpsimd.memset(y[:, 0], 0.0)
                last = nc.gpsimd.memset(y[:, 3], 0.0)
            last.then_inc(edges, 1)
            nc.gpsimd.memset(minus_half[:], -0.5)
            for i in range(2):
                nc.gpsimd.memset(v_sb[i][:, :, C:C + 1], 1.0)
            for m in (ident, ident16, mask16, two_ident):
                nc.gpsimd.memset(m[:], 0.0).then_inc(consts, 1)
            pool.wait_ge(consts, 4)
            for m in (ident, ident16):
                nc.gpsimd.affine_select(out=m[:], in_=m[:], compare_op=ALU.not_equal, fill=1.0, base=0,
                                        pattern=[[-1, P]], channel_multiplier=1).then_inc(consts, 1)
            nc.gpsimd.affine_select(out=mask16[:], in_=mask16[:], compare_op=ALU.is_ge, fill=MASKED, base=0,
                                    pattern=[[0, J], [-1, T]], channel_multiplier=1).then_inc(consts, 1)
            nc.gpsimd.affine_select(out=two_ident[:], in_=two_ident[:], compare_op=ALU.not_equal, fill=1.0,
                                    base=0, pattern=[[-1, C]], channel_multiplier=1).then_inc(consts, 1)
            pool.wait_ge(consts, 8)
            nc.gpsimd.affine_select(out=two_ident[:], in_=two_ident[:], compare_op=ALU.not_equal, fill=1.0,
                                    base=-C, pattern=[[-1, C]], channel_multiplier=1).then_inc(consts, 1)
            pool.wait_ge(w_in, 16 * N_WEIGHTS)

            def step(stages):
                smooth, project, attend, experts, close = stages
                if smooth:
                    c = smooth
                    pool.wait_ge(h_ready, c.count())
                    if c.has_before(2):
                        pool.wait_ge(h2_ready, c.count(back=2))
                    nc.gpsimd.tensor_tensor(hb_sb[c.parity][:], h_sb[c.parity][:],
                                            bv_sb[:].unsqueeze(1).to_broadcast([P, J, C]), ALU.add).then_inc(hb_ready, 1)
                if attend:
                    c = attend
                    pool.wait_ge(ve2_ready, c.count())
                    if c.has_before(1):
                        pool.wait_ge(xh2_ready, c.count(back=1))
                    nc.gpsimd.tensor_tensor(rstd2[:], ve2[:], minus_half[:], ALU.pow).then_inc(rstd2_ready, 1)
                if smooth:
                    c = smooth
                    pool.wait_ge(ve1_ready, c.count())
                    if c.has_before(2):
                        pool.wait_ge(xh1_ready, c.count(back=2))
                    nc.gpsimd.tensor_tensor(rstd1[c.parity][:], ve1[:], minus_half[:], ALU.pow).then_inc(rstd1_ready, 1)
                if experts:
                    c = experts
                    pool.wait_ge(yw_ready, c.count(PAIRS, 2))
                    if c.has_before(1):
                        pool.wait_ge(sum_step, c.count(3, back=1))
                    nc.gpsimd.tensor_tensor(y01[:], yw[0][:], yw[1][:], ALU.add).then_inc(sum_step, 1)
                    pool.wait_ge(yw_ready, c.count(PAIRS, 3))
                    pool.wait_ge(sum_step, c.count(3, 1))
                    nc.gpsimd.tensor_tensor(y012[:], y01[:], yw[2][:], ALU.add).then_inc(sum_step, 1)
                    pool.wait_ge(yw_ready, c.count(PAIRS, 4))
                    pool.wait_ge(sum_step, c.count(3, 2))
                    if c.has_before(1):
                        pool.wait_ge(closed, c.count(back=1))
                    nc.gpsimd.tensor_tensor(y_sum[:], y012[:], yw[3][:], ALU.add).then_inc(sum_step, 1)

            pipeline(pool, TILES, step)

        @block.scalar
        def _(act):
            for half in (slice(0, C), slice(C, P)):
                act.dma_start(wqk[half, 0:DK], wq).then_inc(w_in, 16)
                act.dma_start(wqk[half, DK:2 * DK], wk).then_inc(w_in, 16)
                act.dma_start(wv_sb[half], wv).then_inc(w_in, 16)
                act.dma_start(gamma_sb[half], gamma.unsqueeze(1)).then_inc(w_in, 16)
                act.dma_start(beta_sb[half], beta.unsqueeze(1)).then_inc(w_in, 16)
                act.dma_start(wr_sb[half], wr).then_inc(w_in, 16)
                act.dma_start(w1_sb[half], w1.rearrange("e c h -> c e h")).then_inc(w_in, 16)
            act.dma_start(bqk[0:DK], bq.unsqueeze(1)).then_inc(w_in, 16)
            act.dma_start(bqk[DK:P], bk.unsqueeze(1)).then_inc(w_in, 16)
            act.dma_start(taps_sb[:], taps.unsqueeze(0).to_broadcast([P, 3])).then_inc(w_in, 16)
            act.dma_start(bv_sb[:], bv.unsqueeze(0).to_broadcast([P, C])).then_inc(w_in, 16)
            act.dma_start(br_sb[:], br.unsqueeze(0).to_broadcast([P, E])).then_inc(w_in, 16)
            act.dma_start(w2_sb[:], w2.rearrange("e h c -> h e c")).then_inc(w_in, 16)
            act.dma_start(b1_sb[:], b1.rearrange("e h -> h e")).then_inc(w_in, 16)
            for half in range(2):
                act.dma_start(b2_sb[half * C:(half + 1) * C],
                              b2.rearrange("(p h) c -> h c p", h=2)[half]).then_inc(w_in, 16)
            act.wait_ge(w_in, 16 * (N_WEIGHTS + 3))
            act.wait_ge(w_ready, 1)

            def gelu(c, e):
                act.wait_ge(hidden_done, c.count(E, e + 1))
                if e >= 4:
                    act.wait_ge(expert_done, c.count(PAIRS, (e - 4) // 2 + 1))
                elif c.has_before(1):
                    act.wait_ge(expert_done, c.count(PAIRS, 2 + e // 2 + 1, back=1))
                nc.scalar.activation(g_sb[e % 4][:], hidden[e % 2][:], ACT.Gelu,
                                     bias=b1_f[:, e:e + 1]).then_inc(g_ready, 1)

            def step(stages):
                smooth, project, attend, experts, close = stages
                if attend:
                    c = attend
                    act.wait_ge(top_ready, c.count())
                    if c.has_before(1):
                        act.wait_ge(probs_turned, c.count(back=1))
                    for j in range(J):
                        last = nc.scalar.activation(probs[:, j], mixed[:, j * T:(j + 1) * T], ACT.Exp,
                                                    bias=top[c.parity][:, j:j + 1])
                    last.then_inc(probs_ready, 1)
                if project:
                    c = project
                    act.wait_ge(x1_turned, c.count())
                    if c.has_before(1):
                        act.wait_ge(v_done, c.count(back=1))
                    nc.scalar.activation(x1t[:], turned[:], ACT.Copy).then_inc(x1t_ready, 1)
                if attend:
                    c = attend
                    act.wait_ge(probs_turned, c.count())
                    if c.has_before(1):
                        act.wait_ge(attn_done, c.count(back=1))
                    nc.scalar.activation(probs_t[:].rearrange("p j t -> p (j t)"), turned[:], ACT.Copy).then_inc(probs_t_ready, 1)
                if experts:
                    gelu(experts, 0)
                if project:
                    c = project
                    act.wait_ge(qk_done, c.count())
                    if c.has_before(1):
                        act.wait_ge(scores_done, c.count(back=1))
                    nc.scalar.activation(qt[:], mixed[0:DK], ACT.Identity, bias=bqk[0:DK], scale=SCALE)
                    nc.scalar.activation(kt[:], mixed[DK:P], ACT.Identity, bias=bqk[DK:P]).then_inc(qk_ready, 1)
                    act.wait_ge(v_done, c.count())
                    if c.has_before(1):
                        act.wait_ge(v_ready, c.count(back=1))
                    nc.scalar.activation(v_part[:], values[:].rearrange("p (j s c) -> p j s c", j=J, s=2)[:, :, 0],
                                         ACT.Copy).then_inc(v_part_ready, 1)
                if experts:
                    for e in range(1, 4):
                        gelu(experts, e)
                if attend:
                    c = attend
                    act.wait_ge(x2_turned, c.count())
                    if c.has_before(2):
                        act.wait_ge(hidden_done, c.count(E, back=2))
                    nc.scalar.activation(x2t[c.parity][:], turned[:], ACT.Copy).then_inc(x2t_ready, 1)
                if experts:
                    gelu(experts, 4)
                    gelu(experts, 5)
                if attend:
                    c = attend
                    act.wait_ge(gap_ready, c.count())
                    nc.scalar.activation(tanh_gap[:], gap[:], ACT.Tanh, scale=0.5).then_inc(tanh_ready, 1)
                if experts:
                    gelu(experts, 6)
                    gelu(experts, 7)

            pipeline(act, TILES, step)

        @block.vector
        def _(dve):
            V = nc.vector
            for e in range(E):
                V.memset(iota[:, e:e + 1], float(e))
            dve.wait_ge(w_in, 16 * (N_WEIGHTS + 3))
            V.tensor_scalar(bqk[0:DK], bqk[0:DK], SCALE, None, ALU.mult)
            V.tensor_copy(beta_row[:], beta_sb[0:C].to_broadcast([C, P])).then_inc(folded, 1)
            V.tensor_copy(wqk_hi[:], wqk[:])
            V.tensor_copy(wv_hl[:, 0], wv_sb[:])
            V.tensor_scalar(wr_g[:], wr_sb[:], gamma_sb[:], None, ALU.mult)
            V.tensor_scalar(w1_g[:], w1_sb[:], gamma_sb[:], None, ALU.mult).then_inc(w_step, 1)
            dve.wait_ge(w_step, 1)
            V.tensor_tensor(wqk_lo[:], wqk[:], wqk_hi[:].bitcast(F32), ALU.subtract)
            V.tensor_tensor(wv_hl[:, 1], wv_sb[:], wv_hl[:, 0].bitcast(F32), ALU.subtract)
            V.tensor_copy(wr_hl[:, 0], wr_g[:])
            V.tensor_copy(w1_hi[:], w1_g[:]).then_inc(w_step, 1)
            dve.wait_ge(w_step, 2)
            V.tensor_tensor(wr_hl[:, 1], wr_g[:], wr_hl[:, 0].bitcast(F32), ALU.subtract)
            V.tensor_tensor(w1_lo[:], w1_g[:], w1_hi[:].bitcast(F32), ALU.subtract)
            dve.wait_ge(folded, 2)
            V.tensor_tensor(b1_f[:], small[:, 0:E], b1_sb[:], ALU.add)
            V.tensor_tensor(br_f[:], small[:, E:2 * E], br_sb[:], ALU.add).then_inc(w_ready, 1)
            dve.wait_ge(w_ready, 1)

            def combine(c, p):
                dve.wait_ge(expert_done, c.count(PAIRS, p + 1))
                if p == 0:
                    dve.wait_ge(w_spread[c.parity], c.turns(32))
                if c.has_before(1):
                    dve.wait_ge(sum_step, c.count(3, max(p, 1), back=1))
                V.scalar_tensor_tensor(out=yw[p][:], in0=expert[p % 2][:], scalar=b2_sb[:, p:p + 1],
                                       in1=w_bc[c.parity][:, p], op0=ALU.add, op1=ALU.mult).then_inc(yw_ready, 1)

            def moments(c, h, stats, stats_ready, mom, mom_ready):
                for j in range(J):
                    last = V.bn_stats(stats[:, j], h[:, j])
                last.then_inc(stats_ready, 1)
                dve.wait_ge(w_ready, 1)
                dve.wait_ge(stats_ready, c.count())
                for j in range(J):
                    last = V.bn_aggr(mom[:, j], stats[:, j])
                last.then_inc(mom_ready, 1)
                dve.wait_ge(mom_ready, c.count())

            def normalize(c, h, mom, rstd, xh, xh_ready, split, hi_ready, split_ready, was_turned):
                for j in range(J):
                    last = V.tensor_scalar(xh[:, j], h[:, j], mom[:, j, 0:1], rstd[:, j:j + 1], ALU.subtract, ALU.mult)
                last.then_inc(xh_ready, 1)
                dve.wait_ge(xh_ready, c.count())
                if c.has_before(1):
                    dve.wait_ge(was_turned, c.count(back=1))
                V.tensor_copy(split[:, :, 0].bitcast(F32R), xh[:]).then_inc(hi_ready, 1)
                dve.wait_ge(hi_ready, c.count())
                V.tensor_tensor(split[:, :, 1], xh[:], split[:, :, 0], ALU.subtract).then_inc(split_ready, 1)

            def step(stages):
                smooth, project, attend, experts, close = stages
                if project:
                    c = project
                    dve.wait_ge(rstd1_ready, c.count())
                    normalize(c, h_sb[c.parity], mom1[c.parity], rstd1[c.parity], xh1, xh1_ready, split1,
                              hi1_ready, split1_ready, x1_turned)
                if smooth:
                    c = smooth
                    if c.fixed and c.n < FIRST:
                        dve.wait_ge(x_first[c.n], 64)
                    else:
                        dve.wait_ge(x_rest, 64)
                    if not c.has_before(1):
                        dve.wait_ge(edges, 2)
                    if c.has_before(2):
                        dve.wait_ge(h_ready, c.count(back=2))
                    mine = bass.ds(J * c.n, J)
                    V.tensor_tensor(y_sb[c.parity][:, 1:3], x_sb[:, 0:2, mine], x_sb[:, 1:3, mine],
                                    ALU.max).then_inc(y_ready, 1)
                if close:
                    c = close
                    dve.wait_ge(closed, c.count())
                    if c.has_before(2):
                        dve.wait_ge(stored[c.parity], c.turns(16, back=2))
                    V.tensor_tensor(o_sb[c.parity][:], expert[0][:, 0:J * C].rearrange("p (j c) -> p j c", j=J),
                                    h2_sb[c.parity][:], ALU.add).then_inc(o_ready, 1)
                if attend:
                    c = attend
                    dve.wait_ge(attn_done, c.count())
                    V.reciprocal(rsum[:], small[:].rearrange("p (j c) -> p j c", j=J)[:, :, C]).then_inc(rsum_ready, 1)
                    dve.wait_ge(rsum_ready, c.count())
                    dve.wait_ge(hb_ready, c.count())
                    if c.has_before(2):
                        dve.wait_ge(o_ready, c.count(back=2))
                    for j in range(J):
                        last = V.scalar_tensor_tensor(out=h2_sb[c.parity][:, j], in0=small[:, j * T:j * T + C],
                                                      scalar=rsum[:, j:j + 1], in1=hb_sb[c.parity][:, j],
                                                      op0=ALU.mult, op1=ALU.add)
                    last.then_inc(h2_ready, 1)
                    dve.wait_ge(h2_ready, c.count())
                    moments(c, h2_sb[c.parity], stats2, stats2_ready, mom2, mom2_ready)
                    V.tensor_scalar(ve2[:], mom2[:, :, 1], 1.0 + EPS, EPS * EPS, ALU.mult, ALU.add).then_inc(ve2_ready, 1)
                if smooth:
                    c = smooth
                    y = y_sb[c.parity]
                    dve.wait_ge(y_shifted[c.parity], c.turns(64))
                    if c.has_before(1):
                        dve.wait_ge(h_ready, c.count(back=1))
                    V.tensor_scalar(z_sb[:], y[:, 0:2], taps_sb[:, 0:1], None, ALU.mult).then_inc(blur_step, 1)
                    for k in (1, 2):
                        dve.wait_ge(blur_step, c.count(3, k))
                        V.scalar_tensor_tensor(out=z_sb[:], in0=y[:, k:k + 2], scalar=taps_sb[:, k:k + 1], in1=z_sb[:],
                                               op0=ALU.mult, op1=ALU.add).then_inc(blur_step, 1)
                    dve.wait_ge(blur_step, c.count(3))
                    if c.has_before(2):
                        dve.wait_ge(hb_ready, c.count(back=2))
                    V.tensor_tensor(h_sb[c.parity][:], z_sb[:, 0], z_sb[:, 1], ALU.max).then_inc(h_ready, 1)
                if experts:
                    combine(experts, 0)
                if attend:
                    c = attend
                    dve.wait_ge(rstd2_ready, c.count())
                    normalize(c, h2_sb[c.parity], mom2, rstd2, xh2, xh2_ready, split2, hi2_ready, split2_ready, x2_turned)
                if smooth:
                    c = smooth
                    dve.wait_ge(h_ready, c.count())
                    moments(c, h_sb[c.parity], stats1, stats1_ready, mom1[c.parity], mom1_ready)
                    if c.has_before(1):
                        dve.wait_ge(rstd1_ready, c.count(back=1))
                    V.tensor_scalar(ve1[:], mom1[c.parity][:, :, 1], EPS, None, ALU.add).then_inc(ve1_ready, 1)
                if project:
                    c = project
                    dve.wait_ge(v_part_ready, c.count())
                    if c.has_before(2):
                        dve.wait_ge(attn_done, c.count(back=2))
                    V.tensor_tensor(v_sb[c.parity][:, :, 0:C], values[:].rearrange("p (j s c) -> p j s c", j=J, s=2)[:, :, 1],
                                    v_part[:], ALU.add).then_inc(v_ready, 1)
                if attend:
                    c = attend
                    logits = small[:].rearrange("p (j c) -> p j c", j=J)
                    dve.wait_ge(lg_done, c.count())
                    V.tensor_tensor(lg_part[:], logits[:, :, 0:E], br_f[:].unsqueeze(1).to_broadcast([P, J, E]),
                                    ALU.add).then_inc(lg_step, 1)
                    dve.wait_ge(lg_step, c.count(2, 1))
                    V.tensor_tensor(lg[:], logits[:, :, E:2 * E], lg_part[:], ALU.add).then_inc(lg_step, 1)
                    dve.wait_ge(lg_step, c.count(2))
                if experts:
                    combine(experts, 1)
                if attend:
                    c = attend
                    for j in range(J):
                        last = V.max(best[:, j], lg[:, j])
                    last.then_inc(route_step, 1)
                    dve.wait_ge(route_step, c.count(5, 1))
                    V.tensor_tensor(gap[:], best[:, :, 0], best[:, :, 1], ALU.subtract).then_inc(gap_ready, 1)
                    for j in range(J):
                        last = V.max_index(which[:, j], best[:, j], lg[:, j])
                    last.then_inc(route_step, 1)
                    dve.wait_ge(route_step, c.count(5, 2))
                    V.tensor_copy(which_f[:], which[:, :, 0:2]).then_inc(route_step, 1)
                    dve.wait_ge(route_step, c.count(5, 3))
                if experts:
                    combine(experts, 2)
                if attend:
                    c = attend
                    for s in range(2):
                        V.tensor_tensor(hot[:, s], iota[:].unsqueeze(1).to_broadcast([P, J, E]),
                                        which_f[:, :, s:s + 1].to_broadcast([P, J, E]), ALU.is_equal)
                    dve.wait_ge(tanh_ready, c.count())
                    V.tensor_scalar(share[:, 0], tanh_gap[:], 0.5, 0.5, ALU.mult, ALU.add)
                    V.tensor_scalar(share[:, 1], tanh_gap[:], -0.5, 0.5, ALU.mult, ALU.add).then_inc(route_step, 1)
                    dve.wait_ge(route_step, c.count(5, 4))
                    V.tensor_tensor(hot_w[:], hot[:], share[:].unsqueeze(3).to_broadcast([P, 2, J, E]),
                                    ALU.mult).then_inc(route_step, 1)
                    dve.wait_ge(route_step, c.count(5))
                    if c.has_before(1):
                        dve.wait_ge(w_turned, c.count(back=1))
                    V.tensor_tensor(w_sb[:].rearrange("p e j -> p j e"), hot_w[:, 0], hot_w[:, 1],
                                    ALU.add).then_inc(w_sb_ready, 1)
                if project:
                    c = project
                    dve.wait_ge(scores_done, c.count())
                    if c.has_before(2):
                        dve.wait_ge(probs_ready, c.count(back=2))
                    V.tensor_reduce(top[c.parity][:], mixed[:].rearrange("p (j t) -> p j t", j=J), AX.X, ALU.max,
                                    negate=True).then_inc(top_ready, 1)
                if attend:
                    c = attend
                    dve.wait_ge(w_turned, c.count())
                    if c.has_before(1):
                        dve.wait_ge(w_spilled[1 - c.parity], c.turns(16, back=1))
                    V.tensor_copy(w_t[:], small[0:E * J, 0:T]).then_inc(w_t_ready, 1)
                if experts:
                    combine(experts, 3)

            pipeline(dve, TILES, step)

        @block.tensor
        def _(pe):
            MM = nc.tensor.matmul
            pe.wait_ge(folded, 1)
            for e in range(E):
                MM(small[:, e:e + 1], w1_sb[0:C, e], beta_sb[0:C], start=True, stop=True)
            MM(small[:, E:2 * E], beta_row[:], wr_sb[0:C], start=True, stop=True).then_inc(folded, 1)
            pe.wait_ge(w_ready, 1)
            pe.wait_ge(consts, 9)

            def up(c, e):
                pe.wait_ge(x2t_ready, c.count())
                if e >= 2:
                    pe.wait_ge(g_ready, c.count(E, e - 1))
                elif c.has_before(1):
                    pe.wait_ge(g_ready, c.count(E, E - 1 + e, back=1))
                x2 = x2t[c.parity][:]
                MM(hidden[e % 2][:], w1_hi[:, e], x2, start=True, stop=False)
                MM(hidden[e % 2][:], w1_lo[:, e], x2, start=False, stop=True).then_inc(hidden_done, 1)

            def down(c, p):
                pe.wait_ge(g_ready, c.count(E, 2 * p + 2))
                if p >= 2:
                    pe.wait_ge(yw_ready, c.count(PAIRS, p - 1))
                elif c.has_before(1):
                    pe.wait_ge(yw_ready, c.count(PAIRS, PAIRS - 1 + p, back=1))
                    if p == 0:
                        pe.wait_ge(o_ready, c.count(back=1))
                for half in range(2):
                    e = 2 * p + half
                    last = MM(expert[p % 2][half * C:(half + 1) * C], w2_sb[:, e], g_sb[e % 4][:], start=True, stop=True)
                last.then_inc(expert_done, 1)

            def turn(blocks, done):
                for j in range(J):
                    last = nc.tensor.transpose(turned[:, j * T:(j + 1) * T], blocks[:, j], ident[:])
                last.then_inc(done, 1)

            def step(stages):
                smooth, project, attend, experts, close = stages
                if experts:
                    up(experts, 0)
                    up(experts, 1)
                if project:
                    c = project
                    pe.wait_ge(split1_ready, c.count())
                    if c.has_before(2):
                        pe.wait_ge(x2t_ready, c.count(back=2))
                    turn(split1[:].rearrange("p j s c -> p j (s c)"), x1_turned)
                if close:
                    c = close
                    pe.wait_ge(sum_step, c.count(3))
                    for j in range(J):
                        last = MM(expert[0][:, j * C:(j + 1) * C], y_sum[:, j * T:(j + 1) * T], two_ident[:],
                                  start=True, stop=True)
                    last.then_inc(closed, 1)
                if attend:
                    c = attend
                    pe.wait_ge(probs_ready, c.count())
                    if project:
                        pe.wait_ge(x1t_ready, project.count())
                    turn(probs[:], probs_turned)
                if project:
                    c = project
                    pe.wait_ge(x1t_ready, c.count())
                    if c.has_before(1):
                        pe.wait_ge(probs_ready, c.count(back=1))
                    MM(mixed[:], wqk_hi[:], x1t[:], start=True, stop=False)
                    MM(mixed[:], wqk_lo[:], x1t[:], start=False, stop=True).then_inc(qk_done, 1)
                    if c.has_before(1):
                        pe.wait_ge(v_ready, c.count(back=1))
                    for j in range(J):
                        last = MM(values[:, j * T:(j + 1) * T], x1t[:, j * T:(j + 1) * T],
                                  wv_hl[:].rearrange("p s c -> p (s c)"), start=True, stop=True)
                    last.then_inc(v_done, 1)
                if attend:
                    c = attend
                    pe.wait_ge(probs_t_ready, c.count())
                    pe.wait_ge(v_ready, c.count())
                    if c.has_before(1):
                        pe.wait_ge(w_t_ready, c.count(back=1))
                    for j in range(J):
                        last = MM(small[:, j * T:j * T + C + 1], probs_t[:, j], v_sb[c.parity][:, j], start=True, stop=True)
                    last.then_inc(attn_done, 1)
                if experts:
                    up(experts, 2)
                    down(experts, 0)
                if project:
                    c = project
                    pe.wait_ge(qk_ready, c.count())
                    MM(mixed[:], ident16[:], mask16[:].rearrange("p j t -> p (j t)"), start=True, stop=False,
                       skip_group_check=True)
                    for j in range(J):
                        one = slice(j * T, (j + 1) * T)
                        last = MM(mixed[:, one], qt[:, one], kt[:, one], start=False, stop=True, skip_group_check=True)
                    last.then_inc(scores_done, 1)
                if experts:
                    up(experts, 3)
                    up(experts, 4)
                    down(experts, 1)
                if attend:
                    c = attend
                    pe.wait_ge(split2_ready, c.count())
                    pe.wait_ge(probs_t_ready, c.count())
                    turn(split2[:].rearrange("p j s c -> p j (s c)"), x2_turned)
                if experts:
                    up(experts, 5)
                if attend:
                    c = attend
                    pe.wait_ge(x2t_ready, c.count())
                    pe.wait_ge(h2_ready, c.count())
                    for j in range(J):
                        last = MM(small[:, j * T:j * T + 2 * E], x2t[c.parity][:, j * T:(j + 1) * T],
                                  wr_hl[:].rearrange("p s e -> p (s e)"), start=True, stop=True)
                    last.then_inc(lg_done, 1)
                if experts:
                    up(experts, 6)
                    down(experts, 2)
                if attend:
                    c = attend
                    pe.wait_ge(w_sb_ready, c.count())
                    nc.tensor.transpose(small[0:E * J, 0:T], w_sb[:].rearrange("p e j -> p (e j)"), ident[:]).then_inc(w_turned, 1)
                if experts:
                    up(experts, 7)
                    down(experts, 3)

            pipeline(pe, TILES, step)


_INS = ["x", "L0_tok_blur_kernel", "L0_attn_Wq", "L0_attn_bq", "L0_attn_Wk", "L0_attn_bk", "L0_attn_Wv", "L0_attn_bv",
        "L0_ffn_gamma", "L0_ffn_beta", "L0_ffn_Wr", "L0_ffn_br", "L0_ffn_W1", "L0_ffn_b1", "L0_ffn_W2", "L0_ffn_b2"]


def kernel(**inputs):
    import numpy as np
    import concourse.bacc as bacc
    from concourse.bass_utils import run_bass_kernel_spmd

    nc = bacc.Bacc("TRN2", target_bir_lowering=False, num_devices=1)
    arrays, args = {}, []
    for name in _INS:
        a = np.ascontiguousarray(inputs[name])
        arrays[f"in_{name}"] = a
        args.append(nc.dram_tensor(f"in_{name}", a.shape, mybir.dt.from_np(a.dtype), kind="ExternalInput").ap())
    batch, time, channels = inputs["x"].shape
    out = nc.dram_tensor("out", (batch, time // 2, channels), F32, kind="ExternalOutput").ap()
    w_dram = nc.dram_tensor("w_dram", (2, 8 * 512), F32, kind="Internal").ap()
    audio_tower(nc, *args, out, w_dram)
    return run_bass_kernel_spmd(nc, [arrays], core_ids=[0]).results[0]["out"]
```

```python
from contextlib import ExitStack

import concourse.bass as bass
from concourse import mybir

ALU = mybir.AluOpType
ACT = mybir.ActivationFunctionType
AX = mybir.AxisListType
F32 = mybir.dt.float32
F32R = mybir.dt.float32r
BF16 = mybir.dt.bfloat16
U32 = mybir.dt.uint32

P = 128
STAGES = 5


class Tile:

    def __init__(self, i, offset):
        self.i, self.offset = i, offset
        self.parity = offset % 2
        self.n = 2 * i + offset
        self.fixed = isinstance(i, int)

    def has_before(self, back):
        return self.offset >= back

    def count(self, per=1, k=None, back=0):
        return per * (self.n - back) + (per if k is None else k)

    def turns(self, per, back=0):
        return per * (self.i + (self.offset - back) // 2 + 1)


def pipeline(engine, tiles, step):

    def fixed(k):
        return [Tile(0, k - s) if 0 <= k - s < tiles else None for s in range(STAGES)]

    first = STAGES - 1
    full = tiles - first
    assert full % 2 == 0 and first % 2 == 0
    for k in range(first):
        step(fixed(k))
    with engine.Fori(0, full // 2) as i:
        for odd in range(2):
            step([Tile(i, first + odd - s) for s in range(STAGES)])
    for k in range(tiles, tiles + first):
        step(fixed(k))


def audio_tower(nc, x, taps, wq, bq, wk, bk, wv, bv, gamma, beta, wr, br, w1, b1, w2, b2, out, w_dram):
    BATCH, TIME, C = x.shape
    T = TIME // 2
    E, _, H = w1.shape
    J = 4
    TILES = BATCH // J
    N = J * T
    PAIRS = E // 2
    DK = wq.shape[1]
    SCALE = float(DK) ** -0.5
    EPS = 1e-5
    MASKED = -1e32
    LOWEST = -3.0e38
    EARLY = 6
    assert T == P and 2 * C == P and H == P and N == 512 and DK == C and E == 8

    with ExitStack() as ctx:
        ctx.enter_context(nc.allow_non_contiguous_dma(reason="biases of a few KiB, loaded once"))

        def sb(name, shape, dt=F32):
            return ctx.enter_context(nc.sbuf_tensor(name, shape, dt))

        def bank(name):
            return ctx.enter_context(nc.psum_tensor(name, [P, 512], F32))

        def sem(name):
            return ctx.enter_context(nc.semaphore(name))

        ident = sb("ident", [P, P])
        ident16 = sb("ident16", [P, P], BF16)
        mask16 = sb("mask16", [P, J, T], BF16)
        two_ident = sb("two_ident", [P, C])
        iota = sb("iota", [P, E])
        minus_half = sb("minus_half", [P, J])

        taps_sb = sb("taps_sb", [P, 3])
        wqk = sb("wqk", [P, 2 * DK])
        wqk_hi = sb("wqk_hi", [P, 2 * DK], F32R)
        wqk_lo = sb("wqk_lo", [P, 2 * DK], F32R)
        bqk = sb("bqk", [P, 1])
        wv_sb = sb("wv_sb", [P, C])
        wv_hl = sb("wv_hl", [P, 2, C], F32R)
        bv_sb = sb("bv_sb", [P, C])
        gamma_sb = sb("gamma_sb", [P, 1])
        beta_sb = sb("beta_sb", [P, 1])
        beta_row = sb("beta_row", [C, P])
        wr_sb = sb("wr_sb", [P, E])
        wr_g = sb("wr_g", [P, E])
        wr_hl = sb("wr_hl", [P, 2, E], F32R)
        br_sb = sb("br_sb", [P, E])
        br_f = sb("br_f", [P, E])
        w1_sb = sb("w1_sb", [P, E, H])
        w1_g = sb("w1_g", [P, E, H])
        w1_hi = sb("w1_hi", [P, E, H], F32R)
        w1_lo = sb("w1_lo", [P, E, H], F32R)
        b1_sb = sb("b1_sb", [P, E])
        b1_f = sb("b1_f", [P, E])
        w2_sb = sb("w2_sb", [P, E, C])
        b2_sb = sb("b2_sb", [P, PAIRS])

        x_sb = sb("x_sb", [P, BATCH, 3, C])
        y_all = sb("y_all", [P, 4, BATCH, C])
        z_sb = sb("z_sb", [P, 2, J, C])
        h_sb = [sb(f"h_sb{i}", [P, J, C]) for i in range(2)]
        hb_sb = [sb(f"hb_sb{i}", [P, J, C]) for i in range(2)]
        h2_sb = sb("h2_sb", [P, J, C])
        h2_all = sb("h2_all", [P, BATCH, C])
        stats1 = sb("stats1", [P, J, 6])
        mom1 = sb("mom1", [P, J, 2])
        ve1 = sb("ve1", [P, J])
        rstd1 = sb("rstd1", [P, J])
        centred1 = sb("centred1", [P, J, C])
        xh1 = sb("xh1", [P, J, C])
        split1 = sb("split1", [P, J, 2, C])
        x1t = sb("x1t", [P, N], F32R)
        qt = sb("qt", [DK, N])
        kt = sb("kt", [DK, N])
        v_part = sb("v_part", [P, J, C])
        v_sb = [sb(f"v_sb{i}", [P, J, C + 1]) for i in range(2)]
        top = [sb(f"top{i}", [P, J]) for i in range(2)]
        probs = sb("probs", [P, J, T])
        probs_t = sb("probs_t", [P, J, T])
        rsum = sb("rsum", [P, J])
        stats2 = sb("stats2", [P, J, 6])
        mom2 = sb("mom2", [P, J, 2])
        ve2 = sb("ve2", [P, J])
        rstd2 = sb("rstd2", [P, J])
        centred2 = sb("centred2", [P, J, C])
        xh2 = sb("xh2", [P, J, C])
        split2 = sb("split2", [P, J, 2, C])
        x2t = [sb(f"x2t{i}", [P, N], F32R) for i in range(2)]
        lg_part = sb("lg_part", [P, J, E])
        lg = sb("lg", [P, J, E])
        best = sb("best", [P, J, 8])
        which = sb("which", [P, J, 8], U32)
        which_f = sb("which_f", [P, J, 2])
        gap = sb("gap", [P, J])
        tanh_gap = sb("tanh_gap", [P, J])
        share = sb("share", [P, 2, J])
        hot = sb("hot", [P, 2, J, E])
        hot_w = sb("hot_w", [P, 2, J, E])
        w_sb = sb("w_sb", [P, E, J])
        w_t = sb("w_t", [E * J, T])
        w_bc = [sb(f"w_bc{i}", [P, PAIRS, N]) for i in range(2)]
        g_sb = [sb(f"g_sb{i}", [P, N]) for i in range(E)]
        yw = [sb(f"yw{i}", [P, N]) for i in range(PAIRS)]
        y01 = sb("y01", [P, N])
        y012 = sb("y012", [P, N])
        y_sum = sb("y_sum", [P, N])

        turned = bank("turned")
        mixed = bank("mixed")
        values = bank("values")
        small = bank("small")
        hidden = [bank(f"hidden{i}") for i in range(2)]
        expert = [bank(f"expert{i}") for i in range(2)]

        taps_in = sem("taps_in")
        attn_in = sem("attn_in")
        ffn_in = sem("ffn_in")
        x_ends = sem("x_ends")
        x_in = [sem(f"x_in{i}") for i in range(4)]
        edges = sem("edges")
        consts = sem("consts")
        folded = sem("folded")
        attn_w_ready = sem("attn_w_ready")
        ffn_w_ready = sem("ffn_w_ready")
        w_step = sem("w_step")
        y_ready = sem("y_ready")
        y_shifted = [sem(f"y_shifted{i}") for i in range(4)]
        blur_step = sem("blur_step")
        h_ready = sem("h_ready")
        hb_ready = sem("hb_ready")
        stats1_ready = sem("stats1_ready")
        mom1_ready = sem("mom1_ready")
        ve1_ready = sem("ve1_ready")
        rstd1_ready = sem("rstd1_ready")
        centred1_ready = sem("centred1_ready")
        xh1_ready = sem("xh1_ready")
        hi1_ready = sem("hi1_ready")
        split1_ready = sem("split1_ready")
        x1_turned = sem("x1_turned")
        x1t_ready = sem("x1t_ready")
        qk_done = sem("qk_done")
        v_done = sem("v_done")
        qk_ready = sem("qk_ready")
        v_part_ready = sem("v_part_ready")
        v_ready = sem("v_ready")
        scores_done = sem("scores_done")
        top_ready = sem("top_ready")
        probs_ready = sem("probs_ready")
        probs_turned = sem("probs_turned")
        probs_t_ready = sem("probs_t_ready")
        attn_done = sem("attn_done")
        rsum_ready = sem("rsum_ready")
        h2_ready = sem("h2_ready")
        h2_kept = sem("h2_kept")
        stats2_ready = sem("stats2_ready")
        mom2_ready = sem("mom2_ready")
        ve2_ready = sem("ve2_ready")
        rstd2_ready = sem("rstd2_ready")
        centred2_ready = sem("centred2_ready")
        xh2_ready = sem("xh2_ready")
        hi2_ready = sem("hi2_ready")
        split2_ready = sem("split2_ready")
        x2_turned = sem("x2_turned")
        x2t_ready = sem("x2t_ready")
        lg_done = sem("lg_done")
        lg_step = sem("lg_step")
        gap_ready = sem("gap_ready")
        tanh_ready = sem("tanh_ready")
        route_step = sem("route_step")
        w_sb_ready = sem("w_sb_ready")
        w_turned = sem("w_turned")
        w_t_ready = sem("w_t_ready")
        w_spilled = [sem(f"w_spilled{i}") for i in range(2)]
        w_spread = [sem(f"w_spread{i}") for i in range(2)]
        hidden_done = sem("hidden_done")
        g_ready = sem("g_ready")
        expert_done = sem("expert_done")
        yw_ready = sem("yw_ready")
        sum_step = sem("sum_step")
        closed = sem("closed")
        o_ready = sem("o_ready")
        stored = sem("stored")

        X_GROUPS = ((0, 1), (1, 2), (2, 4), (4, TILES))
        ATTN_LOADS = 9
        FFN_LOADS = 13

        def tile_of(whole, c):
            return whole[:, bass.ds(J * c.n, J)]

        block = ctx.enter_context(nc.Block())

        @block.sync
        def _(sp):
            rows = x.rearrange("b (t r) c -> t b r c", r=2)

            def load_group(g):
                lo, hi = J * X_GROUPS[g][0], J * X_GROUPS[g][1]
                for a, b in ((0, 112), (112, T - 1)):
                    own = rows[a:b, lo:hi]
                    three = bass.AP(tensor=own.tensor, offset=own.offset, ap=[*own.ap[:2], [1, 3 * C]])
                    sp.dma_start(x_sb[a:b, lo:hi].rearrange("t b r c -> t b (r c)"), three).then_inc(x_in[g], 16)

            def shift_group(g):
                lo, hi = J * X_GROUPS[g][0], J * X_GROUPS[g][1]
                sp.wait_ge(y_ready, g + 1)
                for a, b in ((0, 112), (112, T - 1)):
                    sp.dma_start(y_all[a + 1:b + 1, 0, lo:hi], y_all[a:b, 2, lo:hi]).then_inc(y_shifted[g], 16)
                    sp.dma_start(y_all[a:b, 3, lo:hi], y_all[a + 1:b + 1, 1, lo:hi]).then_inc(y_shifted[g], 16)

            load_group(0)
            sp.dma_start(x_sb[T - 1:T, :, 0:2], rows[T - 1:T]).then_inc(x_ends, 16)
            sp.dma_start(x_sb[T - 1:T, :, 2], rows[T - 1:T, :, 1]).then_inc(x_ends, 16)
            load_group(1)
            sp.wait_ge(edges, 2)
            for g in range(len(X_GROUPS)):
                shift_group(g)
                if g + 2 < len(X_GROUPS):
                    load_group(g + 2)

            def step(stages):
                smooth, project, attend, route, close = stages
                if route:
                    c = route
                    sp.wait_ge(w_t_ready, c.count())
                    sp.dma_start(w_dram[c.parity].rearrange("(a t) -> a t", t=T), w_t[:]).then_inc(w_spilled[c.parity], 16)
                    sp.wait_ge(w_spilled[c.parity], c.turns(16))
                    for half in range(2):
                        sp.dma_start(
                            w_bc[c.parity][half * C:(half + 1) * C],
                            w_dram[c.parity].rearrange("(p h t) -> h p t", h=2, t=N)[half].unsqueeze(0).to_broadcast([C, PAIRS, N]),
                        ).then_inc(w_spread[c.parity], 16)
                if close:
                    c = close
                    sp.wait_ge(o_ready, c.count())
                    sp.dma_start(
                        out.rearrange("(n j) t c -> n t j c", j=J)[bass.ds(c.n, 1), :, :, :].rearrange("n t j c -> (n t) j c")
                        if not c.fixed else out[c.n * J:(c.n + 1) * J].rearrange("j t c -> t j c"),
                        tile_of(h2_all, c)).then_inc(stored, 16)

            pipeline(sp, TILES, step)
            sp.wait_ge(stored, 16 * TILES)

        @block.gpsimd
        def _(pool):
            halves = (slice(0, C), slice(C, P))
            for half in halves:
                pool.dma_start(w1_sb[half], w1.rearrange("e c h -> c e h")).then_inc(ffn_in, 16)
                pool.dma_start(gamma_sb[half], gamma.unsqueeze(1)).then_inc(ffn_in, 16)
                pool.dma_start(beta_sb[half], beta.unsqueeze(1)).then_inc(ffn_in, 16)
                pool.dma_start(wr_sb[half], wr).then_inc(ffn_in, 16)
            pool.dma_start(br_sb[:], br.unsqueeze(0).to_broadcast([P, E])).then_inc(ffn_in, 16)
            pool.dma_start(b1_sb[:], b1.rearrange("e h -> h e")).then_inc(ffn_in, 16)
            pool.dma_start(w2_sb[:], w2.rearrange("e h c -> h e c")).then_inc(ffn_in, 16)
            for i, half in enumerate(halves):
                pool.dma_start(b2_sb[half], b2.rearrange("(p h) c -> h c p", h=2)[i]).then_inc(ffn_in, 16)
            nc.gpsimd.memset(minus_half[:], -0.5)
            for m in (ident, ident16, mask16, two_ident):
                nc.gpsimd.memset(m[:], 0.0).then_inc(consts, 1)
            pool.wait_ge(consts, 4)
            for m in (ident, ident16):
                nc.gpsimd.affine_select(out=m[:], in_=m[:], compare_op=ALU.not_equal, fill=1.0, base=0,
                                        pattern=[[-1, P]], channel_multiplier=1).then_inc(consts, 1)
            nc.gpsimd.affine_select(out=mask16[:], in_=mask16[:], compare_op=ALU.is_ge, fill=MASKED, base=0,
                                    pattern=[[0, J], [-1, T]], channel_multiplier=1).then_inc(consts, 1)
            nc.gpsimd.affine_select(out=two_ident[:], in_=two_ident[:], compare_op=ALU.not_equal, fill=1.0,
                                    base=0, pattern=[[-1, C]], channel_multiplier=1).then_inc(consts, 1)
            pool.wait_ge(consts, 8)
            nc.gpsimd.affine_select(out=two_ident[:], in_=two_ident[:], compare_op=ALU.not_equal, fill=1.0,
                                    base=-C, pattern=[[-1, C]], channel_multiplier=1).then_inc(consts, 1)

            def centre(c, mom, mom_ready, h, centred, centred_ready, ve, ve_ready, rstd, rstd_ready, xh_ready):
                pool.wait_ge(mom_ready, c.count())
                if c.has_before(1):
                    pool.wait_ge(xh_ready, c.count(back=1))
                nc.gpsimd.tensor_tensor(centred[:], h, mom[:, :, 0:1].to_broadcast([P, J, C]),
                                        ALU.subtract).then_inc(centred_ready, 1)
                pool.wait_ge(ve_ready, c.count())
                nc.gpsimd.tensor_tensor(rstd[:], ve[:], minus_half[:], ALU.pow).then_inc(rstd_ready, 1)

            def step(stages):
                smooth, project, attend, route, close = stages
                if project:
                    c = project
                    pool.wait_ge(h_ready, c.count())
                    if not c.has_before(1):
                        pool.wait_ge(attn_in, 16 * ATTN_LOADS)
                    if c.has_before(2):
                        pool.wait_ge(h2_ready, c.count(back=2))
                    nc.gpsimd.tensor_tensor(hb_sb[c.parity][:], h_sb[c.parity][:],
                                            bv_sb[:].unsqueeze(1).to_broadcast([P, J, C]), ALU.add).then_inc(hb_ready, 1)
                if smooth:
                    c = smooth
                    if not c.has_before(1):
                        pool.wait_ge(taps_in, 16)
                    if c.fixed:
                        for g, (lo, hi) in enumerate(X_GROUPS):
                            if c.n == lo:
                                pool.wait_ge(y_shifted[g], 64)
                    else:
                        pool.wait_ge(y_shifted[-1], 64)
                    if c.has_before(1):
                        pool.wait_ge(h_ready, c.count(back=1))
                    nc.gpsimd.tensor_tensor(z_sb[:], y_all[:, 0:2, bass.ds(J * c.n, J)],
                                            taps_sb[:, 0:1].unsqueeze(2).unsqueeze(3).to_broadcast([P, 2, J, C]),
                                            ALU.mult).then_inc(blur_step, 1)
                if close:
                    c = close
                    pool.wait_ge(yw_ready, c.count(PAIRS, 2))
                    nc.gpsimd.tensor_tensor(y01[:], yw[0][:], yw[1][:], ALU.add).then_inc(sum_step, 1)
                    pool.wait_ge(yw_ready, c.count(PAIRS, 3))
                    pool.wait_ge(sum_step, c.count(3, 1))
                    nc.gpsimd.tensor_tensor(y012[:], y01[:], yw[2][:], ALU.add).then_inc(sum_step, 1)
                    pool.wait_ge(yw_ready, c.count(PAIRS, 4))
                    pool.wait_ge(sum_step, c.count(3, 2))
                    nc.gpsimd.tensor_tensor(y_sum[:], y012[:], yw[3][:], ALU.add).then_inc(sum_step, 1)
                if attend:
                    centre(attend, mom2, mom2_ready, h2_sb[:], centred2, centred2_ready, ve2, ve2_ready, rstd2,
                           rstd2_ready, xh2_ready)
                if smooth:
                    centre(smooth, mom1, mom1_ready, h_sb[smooth.parity][:], centred1, centred1_ready, ve1, ve1_ready, rstd1,
                           rstd1_ready, xh1_ready)

            pipeline(pool, TILES, step)

        @block.scalar
        def _(act):
            act.dma_start(taps_sb[:], taps.unsqueeze(0).to_broadcast([P, 3])).then_inc(taps_in, 16)
            halves = (slice(0, C), slice(C, P))
            for half in halves:
                act.dma_start(wqk[half, 0:DK], wq).then_inc(attn_in, 16)
                act.dma_start(wqk[half, DK:2 * DK], wk).then_inc(attn_in, 16)
                act.dma_start(wv_sb[half], wv).then_inc(attn_in, 16)
            act.dma_start(bqk[0:DK], bq.unsqueeze(1)).then_inc(attn_in, 16)
            act.dma_start(bqk[DK:P], bk.unsqueeze(1)).then_inc(attn_in, 16)
            act.dma_start(bv_sb[:], bv.unsqueeze(0).to_broadcast([P, C])).then_inc(attn_in, 16)
            def gelu(c, e):
                act.wait_ge(hidden_done, c.count(E, e + 1))
                if not c.has_before(1) and e == 0:
                    act.wait_ge(ffn_w_ready, 1)
                if c.has_before(1):
                    act.wait_ge(expert_done, c.count(PAIRS, e // 2 + 1, back=1))
                nc.scalar.activation(g_sb[e][:], hidden[e % 2][:], ACT.Gelu, bias=b1_f[:, e:e + 1]).then_inc(g_ready, 1)

            def step(stages):
                smooth, project, attend, route, close = stages
                if route:
                    c = route
                    act.wait_ge(x2_turned, c.count())
                    nc.scalar.activation(x2t[c.parity][:], turned[:], ACT.Copy).then_inc(x2t_ready, 1)
                if close:
                    for e in range(EARLY, E):
                        gelu(close, e)
                if project:
                    c = project
                    act.wait_ge(x1_turned, c.count())
                    if c.has_before(1):
                        act.wait_ge(v_done, c.count(back=1))
                    nc.scalar.activation(x1t[:], turned[:], ACT.Copy).then_inc(x1t_ready, 1)
                if attend:
                    c = attend
                    act.wait_ge(top_ready, c.count())
                    if c.has_before(1):
                        act.wait_ge(probs_turned, c.count(back=1))
                    for j in range(J):
                        nc.scalar.activation(probs[:, j], mixed[:, j * T:(j + 1) * T], ACT.Exp,
                                             bias=top[c.parity][:, j:j + 1]).then_inc(probs_ready, 1)
                if route:
                    c = route
                    act.wait_ge(gap_ready, c.count())
                    nc.scalar.activation(tanh_gap[:], gap[:], ACT.Tanh, scale=0.5).then_inc(tanh_ready, 1)
                if project:
                    c = project
                    act.wait_ge(v_done, c.count())
                    if c.has_before(1):
                        act.wait_ge(v_ready, c.count(back=1))
                    nc.scalar.activation(v_part[:], values[:].rearrange("p (j s c) -> p j s c", j=J, s=2)[:, :, 0],
                                         ACT.Copy).then_inc(v_part_ready, 1)
                if attend:
                    c = attend
                    act.wait_ge(probs_turned, c.count())
                    if c.has_before(1):
                        act.wait_ge(attn_done, c.count(back=1))
                    nc.scalar.activation(probs_t[:].rearrange("p j t -> p (j t)"), turned[:], ACT.Copy).then_inc(probs_t_ready, 1)
                if project:
                    c = project
                    act.wait_ge(qk_done, c.count())
                    if c.has_before(1):
                        act.wait_ge(scores_done, c.count(back=1))
                    nc.scalar.activation(qt[:], mixed[0:DK], ACT.Identity, bias=bqk[0:DK], scale=SCALE)
                    nc.scalar.activation(kt[:], mixed[DK:P], ACT.Identity, bias=bqk[DK:P]).then_inc(qk_ready, 1)
                if route:
                    gelu(route, 0)
                    gelu(route, 1)
                if attend:
                    c = attend
                    act.wait_ge(h2_ready, c.count())
                    nc.scalar.activation(tile_of(h2_all, c), h2_sb[:], ACT.Copy).then_inc(h2_kept, 1)
                if route:
                    for e in range(2, EARLY):
                        gelu(route, e)

            pipeline(act, TILES, step)

        @block.vector
        def _(dve):
            V = nc.vector
            V.memset(y_all[:, 0], 0.0).then_inc(edges, 1)
            V.memset(y_all[:, 3], 0.0).then_inc(edges, 1)
            for e in range(E):
                V.memset(iota[:, e:e + 1], float(e))
            for i in range(2):
                V.memset(v_sb[i][:, :, C:C + 1], 1.0)

            def prepare_attention():
                dve.wait_ge(attn_in, 16 * ATTN_LOADS)
                V.tensor_copy(wqk_hi[:], wqk[:])
                V.tensor_copy(wv_hl[:, 0], wv_sb[:]).then_inc(w_step, 1)
                V.tensor_scalar(bqk[0:DK], bqk[0:DK], SCALE, None, ALU.mult)
                dve.wait_ge(w_step, 1)
                V.tensor_tensor(wqk_lo[:], wqk[:], wqk_hi[:].bitcast(F32), ALU.subtract)
                V.tensor_tensor(wv_hl[:, 1], wv_sb[:], wv_hl[:, 0].bitcast(F32), ALU.subtract).then_inc(attn_w_ready, 1)

            def prepare_experts(part):
                if part == 0:
                    dve.wait_ge(ffn_in, 16 * FFN_LOADS)
                    V.tensor_copy(beta_row[:], beta_sb[0:C].to_broadcast([C, P])).then_inc(folded, 1)
                    V.tensor_scalar(wr_g[:], wr_sb[:], gamma_sb[:], None, ALU.mult)
                    V.tensor_scalar(w1_g[:], w1_sb[:], gamma_sb[:], None, ALU.mult).then_inc(w_step, 1)
                if part == 1:
                    dve.wait_ge(w_step, 2)
                    V.tensor_copy(wr_hl[:, 0], wr_g[:])
                    V.tensor_copy(w1_hi[:], w1_g[:]).then_inc(w_step, 1)
                    dve.wait_ge(folded, 2)
                    V.tensor_tensor(b1_f[:], small[:, 0:E], b1_sb[:], ALU.add)
                    V.tensor_tensor(br_f[:], small[:, E:2 * E], br_sb[:], ALU.add)
                if part == 2:
                    dve.wait_ge(w_step, 3)
                    V.tensor_tensor(wr_hl[:, 1], wr_g[:], wr_hl[:, 0].bitcast(F32), ALU.subtract)
                    V.tensor_tensor(w1_lo[:], w1_g[:], w1_hi[:].bitcast(F32), ALU.subtract).then_inc(ffn_w_ready, 1)

            def pool_pairs(g):
                lo, hi = J * X_GROUPS[g][0], J * X_GROUPS[g][1]
                if g == 0:
                    dve.wait_ge(x_ends, 32)
                dve.wait_ge(x_in[g], 32)
                mine = x_sb[:, lo:hi].rearrange("p b r c -> p r b c")
                V.tensor_tensor(y_all[:, 1:3, lo:hi], mine[:, 0:2], mine[:, 1:3], ALU.max).then_inc(y_ready, 1)

            def combine(c, p):
                dve.wait_ge(expert_done, c.count(PAIRS, p + 1))
                if p == 0:
                    dve.wait_ge(w_spread[c.parity], c.turns(32))
                V.scalar_tensor_tensor(out=yw[p][:], in0=expert[p % 2][:], scalar=b2_sb[:, p:p + 1],
                                       in1=w_bc[c.parity][:, p], op0=ALU.add, op1=ALU.mult).then_inc(yw_ready, 1)

            def statistics(h, stats, stats_ready):
                for j in range(J):
                    last = V.bn_stats(stats[:, j], h[:, j])
                last.then_inc(stats_ready, 1)

            def moments(c, stats, stats_ready, mom, mom_ready, centred_ready):
                dve.wait_ge(edges, 2)
                dve.wait_ge(stats_ready, c.count())
                if c.has_before(1):
                    dve.wait_ge(centred_ready, c.count(back=1))
                for j in range(J):
                    last = V.bn_aggr(mom[:, j], stats[:, j])
                last.then_inc(mom_ready, 1)

            def scale(c, centred, centred_ready, rstd, rstd_ready, xh, xh_ready):
                dve.wait_ge(rstd_ready, c.count())
                dve.wait_ge(centred_ready, c.count())
                V.tensor_tensor(xh[:], centred[:], rstd[:].unsqueeze(2).to_broadcast([P, J, C]), ALU.mult).then_inc(xh_ready, 1)

            def split_hi(c, xh, xh_ready, split, hi_ready, was_turned):
                dve.wait_ge(xh_ready, c.count())
                if c.has_before(1):
                    dve.wait_ge(was_turned, c.count(back=1))
                V.tensor_copy(split[:, :, 0].bitcast(F32R), xh[:]).then_inc(hi_ready, 1)

            def split_lo(c, xh, split, hi_ready, split_ready):
                dve.wait_ge(hi_ready, c.count())
                V.tensor_tensor(split[:, :, 1], xh[:], split[:, :, 0], ALU.subtract).then_inc(split_ready, 1)

            def blur(c, k):
                y = y_all[:, k:k + 2, bass.ds(J * c.n, J)]
                dve.wait_ge(blur_step, c.count(3, k))
                V.scalar_tensor_tensor(out=z_sb[:], in0=y, scalar=taps_sb[:, k:k + 1],
                                       in1=z_sb[:], op0=ALU.mult, op1=ALU.add).then_inc(blur_step, 1)

            def step(stages):
                smooth, project, attend, route, close = stages
                logits = small[:].rearrange("p (j c) -> p j c", j=J)
                if project:
                    scale(project, centred1, centred1_ready, rstd1, rstd1_ready, xh1, xh1_ready)
                if project:
                    split_hi(project, xh1, xh1_ready, split1, hi1_ready, x1_turned)
                    split_lo(project, xh1, split1, hi1_ready, split1_ready)
                if close:
                    combine(close, 0)
                if route:
                    c = route
                    dve.wait_ge(lg_done, c.count())
                    V.tensor_tensor(lg_part[:], logits[:, :, 0:E], br_f[:].unsqueeze(1).to_broadcast([P, J, E]),
                                    ALU.add).then_inc(lg_step, 1)
                if route:
                    c = route
                    dve.wait_ge(lg_step, c.count(2, 1))
                    V.tensor_tensor(lg[:], logits[:, :, E:2 * E], lg_part[:], ALU.add).then_inc(lg_step, 1)
                    dve.wait_ge(lg_step, c.count(2))
                if close:
                    combine(close, 1)
                if route:
                    c = route
                    for j in range(J):
                        last = V.max(best[:, j], lg[:, j])
                    last.then_inc(route_step, 1)
                    dve.wait_ge(route_step, c.count(5, 1))
                    V.tensor_tensor(gap[:], best[:, :, 0], best[:, :, 1], ALU.subtract).then_inc(gap_ready, 1)
                    for j in range(J):
                        last = V.max_index(which[:, j], best[:, j], lg[:, j])
                    last.then_inc(route_step, 1)
                if close:
                    combine(close, 2)
                if route:
                    c = route
                    dve.wait_ge(route_step, c.count(5, 2))
                    V.tensor_copy(which_f[:], which[:, :, 0:2]).then_inc(route_step, 1)
                    dve.wait_ge(route_step, c.count(5, 3))
                    for s in range(2):
                        V.tensor_tensor(hot[:, s], iota[:].unsqueeze(1).to_broadcast([P, J, E]),
                                        which_f[:, :, s:s + 1].to_broadcast([P, J, E]), ALU.is_equal)
                    dve.wait_ge(tanh_ready, c.count())
                    V.tensor_scalar(share[:, 0], tanh_gap[:], 0.5, 0.5, ALU.mult, ALU.add)
                    V.tensor_scalar(share[:, 1], tanh_gap[:], -0.5, 0.5, ALU.mult, ALU.add).then_inc(route_step, 1)
                if project:
                    c = project
                    dve.wait_ge(v_part_ready, c.count())
                    if c.has_before(2):
                        dve.wait_ge(attn_done, c.count(back=2))
                    V.tensor_tensor(v_sb[c.parity][:, :, 0:C], values[:].rearrange("p (j s c) -> p j s c", j=J, s=2)[:, :, 1],
                                    v_part[:], ALU.add).then_inc(v_ready, 1)
                if close:
                    combine(close, 3)
                if route:
                    c = route
                    dve.wait_ge(route_step, c.count(5, 4))
                    V.tensor_tensor(hot_w[:], hot[:], share[:].unsqueeze(3).to_broadcast([P, 2, J, E]),
                                    ALU.mult).then_inc(route_step, 1)
                    dve.wait_ge(route_step, c.count(5))
                    if c.has_before(1):
                        dve.wait_ge(w_turned, c.count(back=1))
                    V.tensor_tensor(w_sb[:].rearrange("p e j -> p j e"), hot_w[:, 0], hot_w[:, 1],
                                    ALU.add).then_inc(w_sb_ready, 1)
                if smooth:
                    blur(smooth, 1)
                if route:
                    c = route
                    dve.wait_ge(w_turned, c.count())
                    if c.has_before(1):
                        dve.wait_ge(w_spilled[1 - c.parity], c.turns(16, back=1))
                    V.tensor_copy(w_t[:], values[0:E * J, 0:T]).then_inc(w_t_ready, 1)
                if attend:
                    c = attend
                    dve.wait_ge(attn_done, c.count())
                    V.reciprocal(rsum[:], small[:].rearrange("p (j c) -> p j c", j=J)[:, :, C]).then_inc(rsum_ready, 1)
                if attend:
                    c = attend
                    dve.wait_ge(rsum_ready, c.count())
                    dve.wait_ge(hb_ready, c.count())
                    if c.has_before(1):
                        dve.wait_ge(h2_kept, c.count(back=1))
                    for j in range(J):
                        last = V.scalar_tensor_tensor(out=h2_sb[:, j], in0=small[:, j * T:j * T + C],
                                                      scalar=rsum[:, j:j + 1], in1=hb_sb[c.parity][:, j],
                                                      op0=ALU.mult, op1=ALU.add)
                    last.then_inc(h2_ready, 1)
                if attend:
                    c = attend
                    dve.wait_ge(h2_ready, c.count())
                    statistics(h2_sb, stats2, stats2_ready)
                if attend:
                    c = attend
                    moments(c, stats2, stats2_ready, mom2, mom2_ready, centred2_ready)
                    dve.wait_ge(mom2_ready, c.count())
                    V.tensor_scalar(ve2[:], mom2[:, :, 1], 1.0 + EPS, EPS * EPS, ALU.mult, ALU.add).then_inc(ve2_ready, 1)
                if smooth:
                    blur(smooth, 2)
                if smooth:
                    c = smooth
                    dve.wait_ge(blur_step, c.count(3))
                    if c.has_before(2):
                        dve.wait_ge(hb_ready, c.count(back=2))
                    V.tensor_tensor(h_sb[c.parity][:], z_sb[:, 0], z_sb[:, 1], ALU.max).then_inc(h_ready, 1)
                if smooth:
                    c = smooth
                    dve.wait_ge(h_ready, c.count())
                    statistics(h_sb[c.parity], stats1, stats1_ready)
                if attend:
                    scale(attend, centred2, centred2_ready, rstd2, rstd2_ready, xh2, xh2_ready)
                if smooth:
                    moments(smooth, stats1, stats1_ready, mom1, mom1_ready, centred1_ready)
                if attend:
                    split_hi(attend, xh2, xh2_ready, split2, hi2_ready, x2_turned)
                if smooth:
                    c = smooth
                    dve.wait_ge(mom1_ready, c.count())
                    if c.has_before(1):
                        dve.wait_ge(rstd1_ready, c.count(back=1))
                    V.tensor_scalar(ve1[:], mom1[:, :, 1], EPS, None, ALU.add).then_inc(ve1_ready, 1)
                if attend:
                    split_lo(attend, xh2, split2, hi2_ready, split2_ready)
                if smooth:
                    c = smooth
                    if c.fixed and c.n + 1 < len(X_GROUPS):
                        pool_pairs(c.n + 1)
                        if c.n == 0:
                            prepare_attention()
                        prepare_experts(c.n)
                if close:
                    c = close
                    dve.wait_ge(closed, c.count())
                    dve.wait_ge(h2_kept, c.count())
                    V.tensor_tensor(tile_of(h2_all, c), values[:, 0:J * C].rearrange("p (j c) -> p j c", j=J),
                                    tile_of(h2_all, c), ALU.add).then_inc(o_ready, 1)
                if project:
                    c = project
                    dve.wait_ge(scores_done, c.count())
                    if c.has_before(2):
                        dve.wait_ge(probs_ready, c.count(J, back=2))
                    V.tensor_reduce(top[c.parity][:], mixed[:].rearrange("p (j t) -> p j t", j=J), AX.X, ALU.max,
                                    negate=True).then_inc(top_ready, 1)

            dve.wait_ge(taps_in, 16)
            pool_pairs(0)
            pipeline(dve, TILES, step)

        @block.tensor
        def _(pe):
            MM = nc.tensor.matmul

            def up(c, e):
                if not c.has_before(1) and e == 0:
                    pe.wait_ge(ffn_w_ready, 1)
                pe.wait_ge(x2t_ready, c.count())
                if e >= 2:
                    pe.wait_ge(g_ready, c.count(E, e - 1))
                elif c.has_before(1):
                    pe.wait_ge(g_ready, c.count(E, E - 1 + e, back=1))
                x2 = x2t[c.parity][:]
                MM(hidden[e % 2][:], w1_hi[:, e], x2, start=True, stop=False)
                MM(hidden[e % 2][:], w1_lo[:, e], x2, start=False, stop=True).then_inc(hidden_done, 1)

            def down(c, p):
                pe.wait_ge(g_ready, c.count(E, 2 * p + 2))
                if p >= 2:
                    pe.wait_ge(yw_ready, c.count(PAIRS, p - 1))
                elif c.has_before(1):
                    pe.wait_ge(yw_ready, c.count(PAIRS, PAIRS - 1 + p, back=1))
                for half in range(2):
                    e = 2 * p + half
                    last = MM(expert[p % 2][half * C:(half + 1) * C], w2_sb[:, e], g_sb[e][:], start=True, stop=True)
                last.then_inc(expert_done, 1)

            def turn(blocks, done):
                for j in range(J):
                    last = nc.tensor.transpose(turned[:, j * T:(j + 1) * T], blocks[:, j], ident[:])
                last.then_inc(done, 1)

            def step(stages):
                smooth, project, attend, route, close = stages
                if smooth and not smooth.has_before(1):
                    pe.wait_ge(folded, 1)
                    for e in range(E):
                        MM(small[:, e:e + 1], w1_sb[0:C, e], beta_sb[0:C], start=True, stop=True)
                    MM(small[:, E:2 * E], beta_row[:], wr_sb[0:C], start=True, stop=True).then_inc(folded, 1)
                    pe.wait_ge(consts, 9)
                if route:
                    c = route
                    pe.wait_ge(split2_ready, c.count())
                    pe.wait_ge(probs_t_ready, c.count())
                    turn(split2[:].rearrange("p j s c -> p j (s c)"), x2_turned)
                if close:
                    for e in range(EARLY, E):
                        up(close, e)
                if route:
                    c = route
                    pe.wait_ge(x2t_ready, c.count())
                    pe.wait_ge(h2_ready, c.count())
                    if not c.has_before(1):
                        pe.wait_ge(ffn_w_ready, 1)
                    for j in range(J):
                        last = MM(small[:, j * T:j * T + 2 * E], x2t[c.parity][:, j * T:(j + 1) * T],
                                  wr_hl[:].rearrange("p s e -> p (s e)"), start=True, stop=True)
                    last.then_inc(lg_done, 1)
                if project:
                    c = project
                    pe.wait_ge(split1_ready, c.count())
                    if c.has_before(2):
                        pe.wait_ge(x2t_ready, c.count(back=2))
                    turn(split1[:].rearrange("p j s c -> p j (s c)"), x1_turned)
                if close:
                    down(close, 2)
                if route:
                    up(route, 0)
                if project:
                    c = project
                    pe.wait_ge(x1t_ready, c.count())
                    if not c.has_before(1):
                        pe.wait_ge(attn_w_ready, 1)
                    for j in range(J):
                        last = MM(values[:, j * T:(j + 1) * T], x1t[:, j * T:(j + 1) * T],
                                  wv_hl[:].rearrange("p s c -> p (s c)"), start=True, stop=True)
                    last.then_inc(v_done, 1)
                if close:
                    down(close, 3)
                if attend:
                    c = attend
                    if project:
                        pe.wait_ge(x1t_ready, project.count())
                    for j in range(J):
                        pe.wait_ge(probs_ready, c.count(J, j + 1))
                        last = nc.tensor.transpose(turned[:, j * T:(j + 1) * T], probs[:, j], ident[:])
                    last.then_inc(probs_turned, 1)
                if project:
                    c = project
                    if c.has_before(1):
                        pe.wait_ge(probs_ready, c.count(J, back=1))
                    MM(mixed[:], wqk_hi[:], x1t[:], start=True, stop=False)
                    MM(mixed[:], wqk_lo[:], x1t[:], start=False, stop=True).then_inc(qk_done, 1)
                if route:
                    up(route, 1)
                if attend:
                    c = attend
                    pe.wait_ge(probs_t_ready, c.count())
                    pe.wait_ge(v_ready, c.count())
                    if c.has_before(1):
                        pe.wait_ge(lg_step, c.count(2, back=1))
                    for j in range(J):
                        last = MM(small[:, j * T:j * T + C + 1], probs_t[:, j], v_sb[c.parity][:, j], start=True, stop=True)
                    last.then_inc(attn_done, 1)
                if route:
                    c = route
                    pe.wait_ge(w_sb_ready, c.count())
                    if project:
                        pe.wait_ge(v_ready, project.count())
                    nc.tensor.transpose(values[0:E * J, 0:T], w_sb[:].rearrange("p e j -> p (e j)"), ident[:]).then_inc(w_turned, 1)
                if project:
                    c = project
                    pe.wait_ge(qk_ready, c.count())
                    MM(mixed[:], ident16[:], mask16[:].rearrange("p j t -> p (j t)"), start=True, stop=False,
                       skip_group_check=True)
                    for j in range(J):
                        one = slice(j * T, (j + 1) * T)
                        last = MM(mixed[:, one], qt[:, one], kt[:, one], start=False, stop=True, skip_group_check=True)
                    last.then_inc(scores_done, 1)
                if route:
                    up(route, 2)
                    up(route, 3)
                    down(route, 0)
                    up(route, 4)
                if close:
                    c = close
                    pe.wait_ge(sum_step, c.count(3))
                    if route:
                        pe.wait_ge(w_t_ready, route.count())
                    for j in range(J):
                        last = MM(values[:, j * C:(j + 1) * C], y_sum[:, j * T:(j + 1) * T], two_ident[:],
                                  start=True, stop=True)
                    last.then_inc(closed, 1)
                if route:
                    up(route, 5)
                    down(route, 1)

            pipeline(pe, TILES, step)


_INS = ["x", "L0_tok_blur_kernel", "L0_attn_Wq", "L0_attn_bq", "L0_attn_Wk", "L0_attn_bk", "L0_attn_Wv", "L0_attn_bv",
        "L0_ffn_gamma", "L0_ffn_beta", "L0_ffn_Wr", "L0_ffn_br", "L0_ffn_W1", "L0_ffn_b1", "L0_ffn_W2", "L0_ffn_b2"]


def kernel(**inputs):
    import numpy as np
    import concourse.bacc as bacc
    from concourse.bass_utils import run_bass_kernel_spmd

    nc = bacc.Bacc("TRN2", target_bir_lowering=False, num_devices=1)
    arrays, args = {}, []
    for name in _INS:
        a = np.ascontiguousarray(inputs[name])
        arrays[f"in_{name}"] = a
        args.append(nc.dram_tensor(f"in_{name}", a.shape, mybir.dt.from_np(a.dtype), kind="ExternalInput").ap())
    batch, time, channels = inputs["x"].shape
    out = nc.dram_tensor("out", (batch, time // 2, channels), F32, kind="ExternalOutput").ap()
    w_dram = nc.dram_tensor("w_dram", (2, 8 * 512), F32, kind="Internal").ap()
    audio_tower(nc, *args, out, w_dram)
    return run_bass_kernel_spmd(nc, [arrays], core_ids=[0]).results[0]["out"]
```

```python
from contextlib import ExitStack

import concourse.bass as bass
from concourse import mybir

ALU = mybir.AluOpType
ACT = mybir.ActivationFunctionType
AX = mybir.AxisListType
F32 = mybir.dt.float32
F32R = mybir.dt.float32r
BF16 = mybir.dt.bfloat16
U32 = mybir.dt.uint32

P = 128
STAGES = 4
PEELED = 4


class Tile:

    def __init__(self, i, offset):
        self.i, self.offset = i, offset
        self.parity = offset % 2
        self.n = 2 * i + offset
        self.fixed = isinstance(i, int)

    def has_before(self, back):
        return self.offset >= back

    def count(self, per=1, k=None, back=0):
        return per * (self.n - back) + (per if k is None else k)

    def turns(self, per, back=0):
        return per * (self.i + (self.offset - back) // 2 + 1)


def pipeline(engine, tiles, step):

    def fixed(k):
        return [Tile(0, k - s) if 0 <= k - s < tiles else None for s in range(STAGES)]

    assert (tiles - PEELED) % 2 == 0 and PEELED % 2 == 0 and PEELED >= STAGES - 1
    for k in range(PEELED):
        step(fixed(k))
    with engine.Fori(0, (tiles - PEELED) // 2) as i:
        for odd in range(2):
            step([Tile(i, PEELED + odd - s) for s in range(STAGES)])
    for k in range(tiles, tiles + STAGES - 1):
        step(fixed(k))


def audio_tower(nc, x, taps, wq, bq, wk, bk, wv, bv, gamma, beta, wr, br, w1, b1, w2, b2, out, w_dram):
    BATCH, TIME, C = x.shape
    T = TIME // 2
    E, _, H = w1.shape
    J = 4
    TILES = BATCH // J
    N = J * T
    PAIRS = E // 2
    DK = wq.shape[1]
    SCALE = float(DK) ** -0.5
    EPS = 1e-5
    MASKED = -1e32
    LOWEST = -3.0e38
    GROUPS = [(J * a, J * b) for a, b in ((0, 1), (1, 2), (2, 4), (4, 6), (6, 8))]
    WIDEST = max(hi - lo for lo, hi in GROUPS)
    EARLY = 6
    assert T == P and 2 * C == P and H == P and N == 512 and DK == C and E == 8

    with ExitStack() as ctx:
        ctx.enter_context(nc.allow_non_contiguous_dma(reason="biases of a few KiB, loaded once"))

        def sb(name, shape, dt=F32):
            return ctx.enter_context(nc.sbuf_tensor(name, shape, dt))

        def bank(name):
            return ctx.enter_context(nc.psum_tensor(name, [P, 512], F32))

        def sem(name):
            return ctx.enter_context(nc.semaphore(name))

        ident = sb("ident", [P, P])
        ident16 = sb("ident16", [P, P], BF16)
        mask16 = sb("mask16", [P, J, T], BF16)
        iota = sb("iota", [P, E])
        minus_half = sb("minus_half", [P, WIDEST])

        taps_sb = sb("taps_sb", [P, 3])
        wqk = sb("wqk", [P, 2 * DK])
        wqk_hi = sb("wqk_hi", [P, 2 * DK], F32R)
        wqk_lo = sb("wqk_lo", [P, 2 * DK], F32R)
        bqk = sb("bqk", [P, 1])
        wv_sb = sb("wv_sb", [P, C])
        wv_hl = sb("wv_hl", [P, 2, C], F32R)
        bv_sb = sb("bv_sb", [P, C])
        gamma_sb = sb("gamma_sb", [P, 1])
        beta_sb = sb("beta_sb", [C, 1])
        beta_row = sb("beta_row", [C, P])
        wr_sb = sb("wr_sb", [P, E])
        wr_g = sb("wr_g", [P, E])
        wr_hl = sb("wr_hl", [P, 2, E], F32R)
        br_sb = sb("br_sb", [P, E])
        br_f = sb("br_f", [P, E])
        w1_sb = sb("w1_sb", [P, E, H])
        w1_g = sb("w1_g", [P, E, H])
        w1_hi = sb("w1_hi", [P, E, H], F32R)
        w1_lo = sb("w1_lo", [P, E, H], F32R)
        b1_sb = sb("b1_sb", [P, E])
        b1_f = sb("b1_f", [P, E])
        w2_sb = sb("w2_sb", [P, E, C])
        b2_sb = sb("b2_sb", [P, PAIRS])

        x_sb = sb("x_sb", [P, BATCH, 3, C])
        y_all = sb("y_all", [P, 4, BATCH, C])
        z_sb = [sb(f"z_sb{i}", [P, 2, WIDEST, C]) for i in range(2)]
        z_terms = sb("z_terms", [P, 2, 2, WIDEST, C])
        h_all = sb("h_all", [P, BATCH, C])
        hb_all = sb("hb_all", [P, BATCH, C])
        h2_sb = sb("h2_sb", [P, J, C])
        h2_all = sb("h2_all", [P, BATCH, C])
        stats1 = sb("stats1", [P, BATCH, 6])
        mom1 = sb("mom1", [P, BATCH, 2])
        ve1 = sb("ve1", [P, BATCH])
        rstd1 = sb("rstd1", [P, BATCH])
        centred1 = sb("centred1", [P, BATCH, C])
        xh1 = sb("xh1", [P, J, C])
        split1 = sb("split1", [P, J, 2, C])
        x1t = sb("x1t", [P, N], F32R)
        qt = sb("qt", [DK, N])
        kt = sb("kt", [DK, N])
        v_part = sb("v_part", [P, J, C])
        v_sb = [sb(f"v_sb{i}", [P, J, C + 1]) for i in range(2)]
        top = [sb(f"top{i}", [P, J]) for i in range(2)]
        probs = sb("probs", [P, J, T])
        probs_t = sb("probs_t", [P, J, T])
        rsum = sb("rsum", [P, J])
        stats2 = sb("stats2", [P, J, 6])
        mom2 = sb("mom2", [P, J, 2])
        ve2 = sb("ve2", [P, J])
        rstd2 = sb("rstd2", [P, J])
        centred2 = sb("centred2", [P, J, C])
        xh2 = sb("xh2", [P, J, C])
        split2 = sb("split2", [P, J, 2, C])
        x2t = [sb(f"x2t{i}", [P, N], F32R) for i in range(2)]
        lg_part = sb("lg_part", [P, J, E])
        lg = sb("lg", [P, J, E])
        best = sb("best", [P, J, 8])
        which = sb("which", [P, J, 8], U32)
        which_f = sb("which_f", [P, J, 2])
        gap = sb("gap", [P, J])
        tanh_gap = sb("tanh_gap", [P, J])
        share = sb("share", [P, 2, J])
        hot = sb("hot", [P, 2, J, E])
        hot_w = sb("hot_w", [P, 2, J, E])
        w_sb = sb("w_sb", [P, E, J])
        w_t = sb("w_t", [E * J, T])
        w_bc = [sb(f"w_bc{i}", [P, PAIRS, N]) for i in range(2)]
        g_sb = [sb(f"g_sb{i}", [P, N]) for i in range(E)]
        yw = [sb(f"yw{i}", [P, N]) for i in range(PAIRS)]
        y01 = sb("y01", [P, N])
        y012 = sb("y012", [P, N])
        o_part = sb("o_part", [P, J, C])
        y_sum = sb("y_sum", [P, N])

        turned = bank("turned")
        mixed = bank("mixed")
        values = bank("values")
        small = bank("small")
        hidden = [bank(f"hidden{i}") for i in range(2)]
        expert = [bank(f"expert{i}") for i in range(2)]

        taps_in = sem("taps_in")
        attn_in = sem("attn_in")
        attn_bias_in = sem("attn_bias_in")
        ffn_in = sem("ffn_in")
        ffn_main_in = sem("ffn_main_in")
        x_ends = sem("x_ends")
        x_in = [sem(f"x_in{i}") for i in range(len(GROUPS))]
        edges = sem("edges")
        consts = sem("consts")
        folded = sem("folded")
        attn_w_ready = sem("attn_w_ready")
        ffn_w_step = sem("ffn_w_step")
        bias_ready = sem("bias_ready")
        ffn_w_ready = sem("ffn_w_ready")
        w_step = sem("w_step")
        y_ready = sem("y_ready")
        y_shifted = [sem(f"y_shifted{i}") for i in range(len(GROUPS))]
        z_terms_ready = sem("z_terms_ready")
        blur_step = [sem(f"blur_step{i}") for i in range(len(GROUPS))]
        h_ready = sem("h_ready")
        hb_ready = sem("hb_ready")
        stats1_ready = sem("stats1_ready")
        mom1_ready = sem("mom1_ready")
        ve1_ready = sem("ve1_ready")
        rstd1_ready = sem("rstd1_ready")
        centred1_ready = sem("centred1_ready")
        xh1_ready = sem("xh1_ready")
        hi1_ready = sem("hi1_ready")
        split1_ready = sem("split1_ready")
        x1_turned = sem("x1_turned")
        x1t_ready = sem("x1t_ready")
        qk_done = sem("qk_done")
        v_done = sem("v_done")
        qk_ready = sem("qk_ready")
        v_part_ready = sem("v_part_ready")
        v_ready = sem("v_ready")
        scores_done = sem("scores_done")
        top_ready = sem("top_ready")
        probs_ready = sem("probs_ready")
        probs_turned = sem("probs_turned")
        probs_t_ready = sem("probs_t_ready")
        attn_done = sem("attn_done")
        rsum_ready = sem("rsum_ready")
        h2_ready = sem("h2_ready")
        h2_kept = sem("h2_kept")
        stats2_ready = sem("stats2_ready")
        mom2_ready = sem("mom2_ready")
        ve2_ready = sem("ve2_ready")
        rstd2_ready = sem("rstd2_ready")
        centred2_ready = sem("centred2_ready")
        xh2_ready = sem("xh2_ready")
        hi2_ready = sem("hi2_ready")
        split2_ready = sem("split2_ready")
        x2_turned = sem("x2_turned")
        x2t_ready = sem("x2t_ready")
        lg_done = sem("lg_done")
        lg_step = sem("lg_step")
        gap_ready = sem("gap_ready")
        tanh_ready = sem("tanh_ready")
        route_step = sem("route_step")
        w_sb_ready = sem("w_sb_ready")
        w_turned = sem("w_turned")
        w_t_ready = sem("w_t_ready")
        w_spilled = [sem(f"w_spilled{i}") for i in range(2)]
        w_spread = [sem(f"w_spread{i}") for i in range(2)]
        hidden_done = sem("hidden_done")
        g_ready = sem("g_ready")
        expert_done = sem("expert_done")
        yw_ready = sem("yw_ready")
        sum_step = sem("sum_step")
        closed = sem("closed")
        o_step = sem("o_step")
        o_ready = sem("o_ready")
        stored = sem("stored")

        ATTN_LOADS, ATTN_BIAS_LOADS = 6, 3
        FFN_LOADS, FFN_MAIN_LOADS = 8, 4

        def tile_of(whole, c):
            return whole[:, bass.ds(J * c.n, J)]

        def groups_for(c):
            return c.n + 1 if c.fixed and c.n < 2 else c.i + c.offset // 2 + 2

        block = ctx.enter_context(nc.Block())

        @block.sync
        def _(sp):
            rows = x.rearrange("b (t r) c -> t b r c", r=2)

            def load_group(g):
                lo, hi = GROUPS[g]
                for a, b in ((0, 112), (112, T - 1)):
                    own = rows[a:b, lo:hi]
                    three = bass.AP(tensor=own.tensor, offset=own.offset, ap=[*own.ap[:2], [1, 3 * C]])
                    sp.dma_start(x_sb[a:b, lo:hi].rearrange("t b r c -> t b (r c)"), three).then_inc(x_in[g], 16)

            def shift_group(g):
                lo, hi = GROUPS[g]
                sp.wait_ge(y_ready, g + 1)
                for a, b in ((0, 112), (112, T - 1)):
                    sp.dma_start(y_all[a + 1:b + 1, 0, lo:hi], y_all[a:b, 2, lo:hi]).then_inc(y_shifted[g], 16)
                    sp.dma_start(y_all[a:b, 3, lo:hi], y_all[a + 1:b + 1, 1, lo:hi]).then_inc(y_shifted[g], 16)

            load_group(0)
            sp.dma_start(x_sb[T - 1:T, :, 0:2], rows[T - 1:T]).then_inc(x_ends, 16)
            sp.dma_start(x_sb[T - 1:T, :, 2], rows[T - 1:T, :, 1]).then_inc(x_ends, 16)
            load_group(1)
            sp.wait_ge(edges, 2)
            shift_group(0)
            load_group(2)
            shift_group(1)
            for half in (slice(0, C), slice(C, P)):
                sp.dma_start(gamma_sb[half], gamma.unsqueeze(1)).then_inc(ffn_in, 16)
                sp.dma_start(wr_sb[half], wr).then_inc(ffn_in, 16)
            sp.dma_start(beta_sb[:], beta.unsqueeze(1)).then_inc(ffn_in, 16)
            sp.dma_start(br_sb[:], br.unsqueeze(0).to_broadcast([P, E])).then_inc(ffn_in, 16)
            for half in range(2):
                sp.dma_start(b2_sb[half * C:(half + 1) * C],
                             b2.rearrange("(p h) c -> h c p", h=2)[half]).then_inc(ffn_in, 16)
            for g in range(3, len(GROUPS)):
                load_group(g)
            for g in range(2, len(GROUPS)):
                shift_group(g)

            def step(stages):
                project, attend, route, close = stages
                if route:
                    c = route
                    sp.wait_ge(w_t_ready, c.count())
                    sp.dma_start(w_dram[c.parity].rearrange("(a t) -> a t", t=T), w_t[:]).then_inc(w_spilled[c.parity], 16)
                    sp.wait_ge(w_spilled[c.parity], c.turns(16))
                    for half in range(2):
                        sp.dma_start(
                            w_bc[c.parity][half * C:(half + 1) * C],
                            w_dram[c.parity].rearrange("(p h t) -> h p t", h=2, t=N)[half].unsqueeze(0).to_broadcast([C, PAIRS, N]),
                        ).then_inc(w_spread[c.parity], 16)
                if close:
                    c = close
                    sp.wait_ge(o_ready, c.count())
                    sp.dma_start(
                        out.rearrange("(n j) t c -> n t j c", j=J)[bass.ds(c.n, 1), :, :, :].rearrange("n t j c -> (n t) j c")
                        if not c.fixed else out[c.n * J:(c.n + 1) * J].rearrange("j t c -> t j c"),
                        tile_of(h2_all, c)).then_inc(stored, 16)

            pipeline(sp, TILES, step)
            sp.wait_ge(stored, 16 * TILES)

        @block.gpsimd
        def _(pool):
            nc.gpsimd.memset(minus_half[:], -0.5)
            for m in (ident, ident16, mask16):
                nc.gpsimd.memset(m[:], 0.0).then_inc(consts, 1)
            pool.wait_ge(consts, 3)
            for m in (ident, ident16):
                nc.gpsimd.affine_select(out=m[:], in_=m[:], compare_op=ALU.not_equal, fill=1.0, base=0,
                                        pattern=[[-1, P]], channel_multiplier=1).then_inc(consts, 1)
            nc.gpsimd.affine_select(out=mask16[:], in_=mask16[:], compare_op=ALU.is_ge, fill=MASKED, base=0,
                                    pattern=[[0, J], [-1, T]], channel_multiplier=1).then_inc(consts, 1)
            pool.dma_start(bqk[0:DK], bq.unsqueeze(1)).then_inc(attn_bias_in, 16)
            pool.dma_start(bqk[DK:P], bk.unsqueeze(1)).then_inc(attn_bias_in, 16)
            pool.dma_start(bv_sb[:], bv.unsqueeze(0).to_broadcast([P, C])).then_inc(attn_bias_in, 16)
            for half in (slice(0, C), slice(C, P)):
                pool.dma_start(w1_sb[half], w1.rearrange("e c h -> c e h")).then_inc(ffn_main_in, 16)
            pool.dma_start(b1_sb[:], b1.rearrange("e h -> h e")).then_inc(ffn_main_in, 16)
            pool.dma_start(w2_sb[:], w2.rearrange("e h c -> h e c")).then_inc(ffn_main_in, 16)
            pool.wait_ge(taps_in, 16)

            def first_term(g):
                lo, hi = GROUPS[g]
                pool.wait_ge(y_shifted[g], 64)
                if g >= 2:
                    pool.wait_ge(h_ready, g - 1)
                nc.gpsimd.tensor_tensor(z_sb[g % 2][:, :, 0:hi - lo], y_all[:, 0:2, lo:hi],
                                        taps_sb[:, 0:1].unsqueeze(2).unsqueeze(3).to_broadcast([P, 2, hi - lo, C]),
                                        ALU.mult).then_inc(blur_step[g], 1)

            def add_terms(g):
                pool.wait_ge(z_terms_ready, 1)
                for k in (1, 2):
                    pool.wait_ge(blur_step[g], k)
                    nc.gpsimd.tensor_tensor(z_sb[g % 2][:], z_sb[g % 2][:], z_terms[:, k - 1], ALU.add).then_inc(blur_step[g], 1)

            def centre_group(g):
                lo, hi = GROUPS[g]
                shape = [P, hi - lo, C]
                pool.wait_ge(mom1_ready, g + 1)
                nc.gpsimd.tensor_tensor(centred1[:, lo:hi], h_all[:, lo:hi], mom1[:, lo:hi, 0:1].to_broadcast(shape),
                                        ALU.subtract).then_inc(centred1_ready, 1)
                pool.wait_ge(ve1_ready, g + 1)
                nc.gpsimd.tensor_tensor(rstd1[:, lo:hi], ve1[:, lo:hi], minus_half[:, 0:hi - lo],
                                        ALU.pow).then_inc(rstd1_ready, 1)
                if g == 0:
                    pool.wait_ge(attn_bias_in, 16 * ATTN_BIAS_LOADS)
                nc.gpsimd.tensor_tensor(hb_all[:, lo:hi], h_all[:, lo:hi], bv_sb[:].unsqueeze(1).to_broadcast(shape),
                                        ALU.add).then_inc(hb_ready, 1)

            def step(stages):
                project, attend, route, close = stages
                peeled = project.n if project and project.fixed else None
                if peeled == 0:
                    centre_group(1)
                    first_term(2)
                    pool.wait_ge(ffn_w_step, 2)
                    nc.gpsimd.tensor_tensor(wr_hl[:, 1], wr_g[:], wr_hl[:, 0].bitcast(F32), ALU.subtract)
                    nc.gpsimd.tensor_tensor(w1_lo[:], w1_g[:], w1_hi[:].bitcast(F32), ALU.subtract).then_inc(ffn_w_ready, 1)
                if close:
                    c = close
                    pool.wait_ge(yw_ready, c.count(PAIRS, 2))
                    nc.gpsimd.tensor_tensor(y01[:], yw[0][:], yw[1][:], ALU.add).then_inc(sum_step, 1)
                    pool.wait_ge(yw_ready, c.count(PAIRS, 3))
                    pool.wait_ge(sum_step, c.count(3, 1))
                    nc.gpsimd.tensor_tensor(y012[:], y01[:], yw[2][:], ALU.add).then_inc(sum_step, 1)
                    pool.wait_ge(yw_ready, c.count(PAIRS, 4))
                    pool.wait_ge(sum_step, c.count(3, 2))
                    nc.gpsimd.tensor_tensor(y_sum[:], y012[:], yw[3][:], ALU.add).then_inc(sum_step, 1)
                if attend:
                    c = attend
                    pool.wait_ge(mom2_ready, c.count())
                    if c.has_before(1):
                        pool.wait_ge(xh2_ready, c.count(back=1))
                    nc.gpsimd.tensor_tensor(centred2[:], h2_sb[:], mom2[:, :, 0:1].to_broadcast([P, J, C]),
                                            ALU.subtract).then_inc(centred2_ready, 1)
                    pool.wait_ge(ve2_ready, c.count())
                    nc.gpsimd.tensor_tensor(rstd2[:], ve2[:], minus_half[:, 0:J], ALU.pow).then_inc(rstd2_ready, 1)
                if peeled in (1, 2, 3):
                    centre_group(peeled + 1)
                if peeled == 1:
                    first_term(3)
                    first_term(4)
                    add_terms(4)

            first_term(0)
            centre_group(0)
            first_term(1)
            pipeline(pool, TILES, step)

        @block.scalar
        def _(act):
            act.dma_start(taps_sb[:], taps.unsqueeze(0).to_broadcast([P, 3])).then_inc(taps_in, 16)
            halves = (slice(0, C), slice(C, P))
            for half in halves:
                act.dma_start(wqk[half, 0:DK], wq).then_inc(attn_in, 16)
                act.dma_start(wqk[half, DK:2 * DK], wk).then_inc(attn_in, 16)
                act.dma_start(wv_sb[half], wv).then_inc(attn_in, 16)
            def gelu(c, e):
                act.wait_ge(hidden_done, c.count(E, e + 1))
                if not c.has_before(1) and e == 0:
                    act.wait_ge(bias_ready, 1)
                if c.has_before(1):
                    act.wait_ge(expert_done, c.count(PAIRS, e // 2 + 1, back=1))
                nc.scalar.activation(g_sb[e][:], hidden[e % 2][:], ACT.Gelu, bias=b1_f[:, e:e + 1]).then_inc(g_ready, 1)

            def multiply_terms(g):
                lo, hi = GROUPS[g]
                act.wait_ge(y_shifted[g], 64)
                for k in (1, 2):
                    last = nc.scalar.activation(z_terms[:, k - 1], y_all[:, k:k + 2, lo:hi], ACT.Identity,
                                                scale=taps_sb[:, k:k + 1])
                last.then_inc(z_terms_ready, 1)

            def step(stages):
                project, attend, route, close = stages
                peeled = project.n if project and project.fixed else None
                if route:
                    c = route
                    act.wait_ge(x2_turned, c.count())
                    nc.scalar.activation(x2t[c.parity][:], turned[:], ACT.Copy).then_inc(x2t_ready, 1)
                if close:
                    for e in range(EARLY, E):
                        gelu(close, e)
                if peeled is not None:
                    c = project
                    act.wait_ge(x1_turned, c.count())
                    if c.has_before(1):
                        act.wait_ge(v_done, c.count(back=1))
                    nc.scalar.activation(x1t[:], turned[:], ACT.Copy).then_inc(x1t_ready, 1)
                if attend:
                    c = attend
                    act.wait_ge(top_ready, c.count())
                    if c.has_before(1):
                        act.wait_ge(probs_turned, c.count(back=1))
                    for j in range(J):
                        nc.scalar.activation(probs[:, j], mixed[:, j * T:(j + 1) * T], ACT.Exp,
                                             bias=top[c.parity][:, j:j + 1]).then_inc(probs_ready, 1)
                if route:
                    c = route
                    act.wait_ge(gap_ready, c.count())
                    nc.scalar.activation(tanh_gap[:], gap[:], ACT.Tanh, scale=0.5).then_inc(tanh_ready, 1)
                if attend:
                    c = attend
                    act.wait_ge(probs_turned, c.count())
                    if c.has_before(1):
                        act.wait_ge(attn_done, c.count(back=1))
                    nc.scalar.activation(probs_t[:].rearrange("p j t -> p (j t)"), turned[:], ACT.Copy).then_inc(probs_t_ready, 1)
                if project:
                    c = project
                    act.wait_ge(qk_done, c.count())
                    if c.has_before(1):
                        act.wait_ge(scores_done, c.count(back=1))
                    nc.scalar.activation(qt[:], mixed[0:DK], ACT.Identity, bias=bqk[0:DK], scale=SCALE)
                    nc.scalar.activation(kt[:], mixed[DK:P], ACT.Identity, bias=bqk[DK:P]).then_inc(qk_ready, 1)
                    act.wait_ge(v_done, c.count())
                    if c.has_before(1):
                        act.wait_ge(v_ready, c.count(back=1))
                    nc.scalar.activation(v_part[:], values[:].rearrange("p (j s c) -> p j s c", j=J, s=2)[:, :, 0],
                                         ACT.Copy).then_inc(v_part_ready, 1)
                if peeled == 0:
                    act.wait_ge(ffn_in, 16 * FFN_LOADS)
                    act.wait_ge(ffn_main_in, 16 * FFN_MAIN_LOADS)
                    nc.scalar.activation(beta_row[:], beta_sb[:].to_broadcast([C, P]), ACT.Copy).then_inc(folded, 1)
                    nc.scalar.activation(wr_g[:], wr_sb[:], ACT.Identity, scale=gamma_sb[:])
                    nc.scalar.activation(w1_g[:], w1_sb[:], ACT.Identity, scale=gamma_sb[:]).then_inc(ffn_w_step, 1)
                    act.wait_ge(ffn_w_step, 1)
                    nc.scalar.activation(wr_hl[:, 0], wr_g[:], ACT.Copy)
                    nc.scalar.activation(w1_hi[:], w1_g[:], ACT.Copy).then_inc(ffn_w_step, 1)
                if route:
                    for e in range(4):
                        gelu(route, e)
                if attend:
                    c = attend
                    act.wait_ge(h2_ready, c.count())
                    nc.scalar.activation(tile_of(h2_all, c), h2_sb[:], ACT.Copy).then_inc(h2_kept, 1)
                if peeled == 1:
                    multiply_terms(4)
                if route:
                    for e in range(4, EARLY):
                        gelu(route, e)

            pipeline(act, TILES, step)

        @block.vector
        def _(dve):
            V = nc.vector
            V.memset(y_all[:, 0], 0.0).then_inc(edges, 1)
            V.memset(y_all[:, 3], 0.0).then_inc(edges, 1)
            for e in range(E):
                V.memset(iota[:, e:e + 1], float(e))
            for i in range(2):
                V.memset(v_sb[i][:, :, C:C + 1], 1.0)

            def prepare_attention():
                dve.wait_ge(attn_in, 16 * ATTN_LOADS)
                dve.wait_ge(attn_bias_in, 16 * ATTN_BIAS_LOADS)
                V.tensor_copy(wqk_hi[:], wqk[:])
                V.tensor_copy(wv_hl[:, 0], wv_sb[:]).then_inc(w_step, 1)
                V.tensor_scalar(bqk[0:DK], bqk[0:DK], SCALE, None, ALU.mult)
                dve.wait_ge(w_step, 1)
                V.tensor_tensor(wqk_lo[:], wqk[:], wqk_hi[:].bitcast(F32), ALU.subtract)
                V.tensor_tensor(wv_hl[:, 1], wv_sb[:], wv_hl[:, 0].bitcast(F32), ALU.subtract).then_inc(attn_w_ready, 1)

            def fold_biases():
                dve.wait_ge(folded, 2)
                V.tensor_tensor(b1_f[:], hidden[0][:, 0:E], b1_sb[:], ALU.add)
                V.tensor_tensor(br_f[:], hidden[0][:, E:2 * E], br_sb[:], ALU.add).then_inc(bias_ready, 1)

            def pool_pairs(g):
                lo, hi = GROUPS[g]
                if g == 0:
                    dve.wait_ge(x_ends, 32)
                dve.wait_ge(x_in[g], 32)
                mine = x_sb[:, lo:hi].rearrange("p b r c -> p r b c")
                V.tensor_tensor(y_all[:, 1:3, lo:hi], mine[:, 0:2], mine[:, 1:3], ALU.max).then_inc(y_ready, 1)

            def combine(c, p):
                dve.wait_ge(expert_done, c.count(PAIRS, p + 1))
                if p == 0:
                    dve.wait_ge(w_spread[c.parity], c.turns(32))
                V.scalar_tensor_tensor(out=yw[p][:], in0=expert[p % 2][:], scalar=b2_sb[:, p:p + 1],
                                       in1=w_bc[c.parity][:, p], op0=ALU.add, op1=ALU.mult).then_inc(yw_ready, 1)

            def add_terms(g):
                lo, hi = GROUPS[g]
                z = z_sb[g % 2][:, :, 0:hi - lo]
                for k in (1, 2):
                    dve.wait_ge(blur_step[g], k)
                    V.scalar_tensor_tensor(out=z, in0=y_all[:, k:k + 2, lo:hi], scalar=taps_sb[:, k:k + 1],
                                           in1=z, op0=ALU.mult, op1=ALU.add).then_inc(blur_step[g], 1)

            def pool_z(g):
                lo, hi = GROUPS[g]
                z = z_sb[g % 2][:, :, 0:hi - lo]
                dve.wait_ge(blur_step[g], 3)
                V.tensor_tensor(h_all[:, lo:hi], z[:, 0], z[:, 1], ALU.max).then_inc(h_ready, 1)

            def moments_of_group(g):
                lo, hi = GROUPS[g]
                dve.wait_ge(h_ready, g + 1)
                for b in range(lo, hi):
                    last = V.bn_stats(stats1[:, b], h_all[:, b])
                last.then_inc(stats1_ready, 1)
                dve.wait_ge(stats1_ready, g + 1)
                for b in range(lo, hi):
                    last = V.bn_aggr(mom1[:, b], stats1[:, b])
                last.then_inc(mom1_ready, 1)
                dve.wait_ge(mom1_ready, g + 1)
                V.tensor_scalar(ve1[:, lo:hi], mom1[:, lo:hi, 1], EPS, None, ALU.add).then_inc(ve1_ready, 1)

            def split_hi(c, xh, xh_ready, split, hi_ready, was_turned):
                dve.wait_ge(xh_ready, c.count())
                if c.has_before(1):
                    dve.wait_ge(was_turned, c.count(back=1))
                V.tensor_copy(split[:, :, 0].bitcast(F32R), xh[:]).then_inc(hi_ready, 1)

            def split_lo(c, xh, split, hi_ready, split_ready):
                dve.wait_ge(hi_ready, c.count())
                V.tensor_tensor(split[:, :, 1], xh[:], split[:, :, 0], ALU.subtract).then_inc(split_ready, 1)

            def step(stages):
                project, attend, route, close = stages
                logits = small[:].rearrange("p (j c) -> p j c", j=J)
                pair_halves = values[:].rearrange("p (j s c) -> p j s c", j=J, s=2)
                peeled = project.n if project and project.fixed else None
                if project:
                    c = project
                    dve.wait_ge(rstd1_ready, groups_for(c))
                    V.tensor_tensor(xh1[:], tile_of(centred1, c), tile_of(rstd1, c).unsqueeze(2).to_broadcast([P, J, C]),
                                    ALU.mult).then_inc(xh1_ready, 1)
                if project:
                    split_hi(project, xh1, xh1_ready, split1, hi1_ready, x1_turned)
                    split_lo(project, xh1, split1, hi1_ready, split1_ready)
                if close:
                    combine(close, 0)
                if route:
                    c = route
                    dve.wait_ge(lg_done, c.count())
                    V.tensor_tensor(lg_part[:], logits[:, :, 0:E], br_f[:].unsqueeze(1).to_broadcast([P, J, E]),
                                    ALU.add).then_inc(lg_step, 1)
                if project and peeled is None:
                    c = project
                    dve.wait_ge(x1_turned, c.count())
                    if c.has_before(1):
                        dve.wait_ge(v_done, c.count(back=1))
                    V.tensor_copy(x1t[:], turned[:]).then_inc(x1t_ready, 1)
                if peeled == 0:
                    pool_pairs(2)
                    add_terms(1)
                    pool_z(1)
                    moments_of_group(1)
                if peeled == 1:
                    add_terms(2)
                    pool_z(2)
                    pool_pairs(3)
                    pool_pairs(4)
                if route:
                    c = route
                    dve.wait_ge(lg_step, c.count(2, 1))
                    V.tensor_tensor(lg[:], logits[:, :, E:2 * E], lg_part[:], ALU.add).then_inc(lg_step, 1)
                    dve.wait_ge(lg_step, c.count(2))
                if close:
                    combine(close, 1)
                if route:
                    c = route
                    for j in range(J):
                        last = V.max(best[:, j], lg[:, j])
                    last.then_inc(route_step, 1)
                if route:
                    c = route
                    dve.wait_ge(route_step, c.count(5, 1))
                    V.tensor_tensor(gap[:], best[:, :, 0], best[:, :, 1], ALU.subtract).then_inc(gap_ready, 1)
                    for j in range(J):
                        last = V.max_index(which[:, j], best[:, j], lg[:, j])
                    last.then_inc(route_step, 1)
                    dve.wait_ge(route_step, c.count(5, 2))
                    V.tensor_copy(which_f[:], which[:, :, 0:2]).then_inc(route_step, 1)
                    dve.wait_ge(route_step, c.count(5, 3))
                    for s in range(2):
                        V.tensor_tensor(hot[:, s], iota[:].unsqueeze(1).to_broadcast([P, J, E]),
                                        which_f[:, :, s:s + 1].to_broadcast([P, J, E]), ALU.is_equal)
                if peeled == 3:
                    pool_z(4)
                if route:
                    c = route
                    dve.wait_ge(tanh_ready, c.count())
                    V.tensor_scalar(share[:, 0], tanh_gap[:], 0.5, 0.5, ALU.mult, ALU.add)
                    V.tensor_scalar(share[:, 1], tanh_gap[:], -0.5, 0.5, ALU.mult, ALU.add).then_inc(route_step, 1)
                if close:
                    combine(close, 2)
                if route:
                    c = route
                    dve.wait_ge(route_step, c.count(5, 4))
                    V.tensor_tensor(hot_w[:], hot[:], share[:].unsqueeze(3).to_broadcast([P, 2, J, E]),
                                    ALU.mult).then_inc(route_step, 1)
                    dve.wait_ge(route_step, c.count(5))
                    if c.has_before(1):
                        dve.wait_ge(w_turned, c.count(back=1))
                    V.tensor_tensor(w_sb[:].rearrange("p e j -> p j e"), hot_w[:, 0], hot_w[:, 1],
                                    ALU.add).then_inc(w_sb_ready, 1)
                if peeled == 2:
                    add_terms(3)
                if close:
                    combine(close, 3)
                if route:
                    c = route
                    dve.wait_ge(w_turned, c.count())
                    if c.has_before(1):
                        dve.wait_ge(w_spilled[1 - c.parity], c.turns(16, back=1))
                    V.tensor_copy(w_t[:], turned[0:E * J, 0:T]).then_inc(w_t_ready, 1)
                if project:
                    c = project
                    dve.wait_ge(v_part_ready, c.count())
                    if c.has_before(2):
                        dve.wait_ge(attn_done, c.count(back=2))
                    V.tensor_tensor(v_sb[c.parity][:, :, 0:C], values[:].rearrange("p (j s c) -> p j s c", j=J, s=2)[:, :, 1],
                                    v_part[:], ALU.add).then_inc(v_ready, 1)
                if attend:
                    c = attend
                    dve.wait_ge(attn_done, c.count())
                    V.reciprocal(rsum[:], small[:].rearrange("p (j c) -> p j c", j=J)[:, :, C]).then_inc(rsum_ready, 1)
                if attend:
                    c = attend
                    dve.wait_ge(rsum_ready, c.count())
                    dve.wait_ge(hb_ready, groups_for(c))
                    if c.has_before(1):
                        dve.wait_ge(h2_kept, c.count(back=1))
                    for j in range(J):
                        last = V.scalar_tensor_tensor(out=h2_sb[:, j], in0=small[:, j * T:j * T + C],
                                                      scalar=rsum[:, j:j + 1], in1=tile_of(hb_all, c)[:, j],
                                                      op0=ALU.mult, op1=ALU.add)
                    last.then_inc(h2_ready, 1)
                if attend:
                    c = attend
                    dve.wait_ge(h2_ready, c.count())
                    for j in range(J):
                        last = V.bn_stats(stats2[:, j], h2_sb[:, j])
                    last.then_inc(stats2_ready, 1)
                if peeled == 2:
                    pool_z(3)
                if attend:
                    c = attend
                    dve.wait_ge(edges, 2)
                    dve.wait_ge(stats2_ready, c.count())
                    if c.has_before(1):
                        dve.wait_ge(centred2_ready, c.count(back=1))
                    for j in range(J):
                        last = V.bn_aggr(mom2[:, j], stats2[:, j])
                    last.then_inc(mom2_ready, 1)
                    dve.wait_ge(mom2_ready, c.count())
                    V.tensor_scalar(ve2[:], mom2[:, :, 1], 1.0 + EPS, EPS * EPS, ALU.mult, ALU.add).then_inc(ve2_ready, 1)
                if close:
                    c = close
                    dve.wait_ge(closed, c.count())
                    dve.wait_ge(h2_kept, c.count())
                    V.tensor_tensor(o_part[:], pair_halves[:, :, 0], tile_of(h2_all, c), ALU.add).then_inc(o_step, 1)
                if peeled in (1, 2, 3):
                    moments_of_group(peeled + 1)
                if project:
                    c = project
                    dve.wait_ge(scores_done, c.count())
                    if c.has_before(2):
                        dve.wait_ge(probs_ready, c.count(J, back=2))
                    V.tensor_reduce(top[c.parity][:], mixed[:].rearrange("p (j t) -> p j t", j=J), AX.X, ALU.max,
                                    negate=True).then_inc(top_ready, 1)
                if close:
                    c = close
                    dve.wait_ge(o_step, c.count())
                    V.tensor_tensor(tile_of(h2_all, c), pair_halves[:, :, 1], o_part[:], ALU.add).then_inc(o_ready, 1)
                if attend:
                    c = attend
                    dve.wait_ge(rstd2_ready, c.count())
                    dve.wait_ge(centred2_ready, c.count())
                    V.tensor_tensor(xh2[:], centred2[:], rstd2[:].unsqueeze(2).to_broadcast([P, J, C]),
                                    ALU.mult).then_inc(xh2_ready, 1)
                    split_hi(c, xh2, xh2_ready, split2, hi2_ready, x2_turned)
                    split_lo(c, xh2, split2, hi2_ready, split2_ready)
                if peeled == 1:
                    fold_biases()

            dve.wait_ge(taps_in, 16)
            pool_pairs(0)
            pool_pairs(1)
            add_terms(0)
            pool_z(0)
            moments_of_group(0)
            prepare_attention()
            pipeline(dve, TILES, step)

        @block.tensor
        def _(pe):
            MM = nc.tensor.matmul

            def up(c, e):
                if not c.has_before(1) and e == 0:
                    pe.wait_ge(ffn_w_ready, 1)
                pe.wait_ge(x2t_ready, c.count())
                if e >= 2:
                    pe.wait_ge(g_ready, c.count(E, e - 1))
                elif c.has_before(1):
                    pe.wait_ge(g_ready, c.count(E, E - 1 + e, back=1))
                x2 = x2t[c.parity][:]
                MM(hidden[e % 2][:], w1_hi[:, e], x2, start=True, stop=False)
                MM(hidden[e % 2][:], w1_lo[:, e], x2, start=False, stop=True).then_inc(hidden_done, 1)

            def down(c, p):
                pe.wait_ge(g_ready, c.count(E, 2 * p + 2))
                if p >= 2:
                    pe.wait_ge(yw_ready, c.count(PAIRS, p - 1))
                elif c.has_before(1):
                    pe.wait_ge(yw_ready, c.count(PAIRS, PAIRS - 1 + p, back=1))
                for half in range(2):
                    e = 2 * p + half
                    last = MM(expert[p % 2][half * C:(half + 1) * C], w2_sb[:, e], g_sb[e][:], start=True, stop=True)
                last.then_inc(expert_done, 1)

            def turn(blocks, done):
                for j in range(J):
                    last = nc.tensor.transpose(turned[:, j * T:(j + 1) * T], blocks[:, j], ident[:])
                last.then_inc(done, 1)

            def step(stages):
                project, attend, route, close = stages
                if route:
                    c = route
                    pe.wait_ge(split2_ready, c.count())
                    pe.wait_ge(probs_t_ready, c.count())
                    if c.has_before(1):
                        pe.wait_ge(w_t_ready, c.count(back=1))
                    turn(split2[:].rearrange("p j s c -> p j (s c)"), x2_turned)
                if close:
                    for e in range(EARLY, E):
                        up(close, e)
                if route:
                    c = route
                    pe.wait_ge(x2t_ready, c.count())
                    pe.wait_ge(h2_ready, c.count())
                    if not c.has_before(1):
                        pe.wait_ge(ffn_w_ready, 1)
                    for j in range(J):
                        last = MM(small[:, j * T:j * T + 2 * E], x2t[c.parity][:, j * T:(j + 1) * T],
                                  wr_hl[:].rearrange("p s e -> p (s e)"), start=True, stop=True)
                    last.then_inc(lg_done, 1)
                if project:
                    c = project
                    pe.wait_ge(split1_ready, c.count())
                    if c.has_before(2):
                        pe.wait_ge(x2t_ready, c.count(back=2))
                    turn(split1[:].rearrange("p j s c -> p j (s c)"), x1_turned)
                if close:
                    down(close, 2)
                if route:
                    up(route, 0)
                if attend:
                    c = attend
                    if project:
                        pe.wait_ge(x1t_ready, project.count())
                    for j in range(J):
                        pe.wait_ge(probs_ready, c.count(J, j + 1))
                        last = nc.tensor.transpose(turned[:, j * T:(j + 1) * T], probs[:, j], ident[:])
                    last.then_inc(probs_turned, 1)
                if project:
                    c = project
                    pe.wait_ge(x1t_ready, c.count())
                    if not c.has_before(1):
                        pe.wait_ge(attn_w_ready, 1)
                    else:
                        pe.wait_ge(probs_ready, c.count(J, back=1))
                    MM(mixed[:], wqk_hi[:], x1t[:], start=True, stop=False)
                    MM(mixed[:], wqk_lo[:], x1t[:], start=False, stop=True).then_inc(qk_done, 1)
                if close:
                    down(close, 3)
                if project:
                    c = project
                    pe.wait_ge(x1t_ready, c.count())
                    if not c.has_before(1):
                        pe.wait_ge(attn_w_ready, 1)
                    for j in range(J):
                        last = MM(values[:, j * T:(j + 1) * T], x1t[:, j * T:(j + 1) * T],
                                  wv_hl[:].rearrange("p s c -> p (s c)"), start=True, stop=True)
                    last.then_inc(v_done, 1)
                if route:
                    c = route
                    pe.wait_ge(w_sb_ready, c.count())
                    if attend:
                        pe.wait_ge(probs_t_ready, attend.count())
                    nc.tensor.transpose(turned[0:E * J, 0:T], w_sb[:].rearrange("p e j -> p (e j)"), ident[:]).then_inc(w_turned, 1)
                if attend:
                    c = attend
                    pe.wait_ge(probs_t_ready, c.count())
                    pe.wait_ge(v_ready, c.count())
                    if c.has_before(1):
                        pe.wait_ge(lg_step, c.count(2, back=1))
                    for j in range(J):
                        last = MM(small[:, j * T:j * T + C + 1], probs_t[:, j], v_sb[c.parity][:, j], start=True, stop=True)
                    last.then_inc(attn_done, 1)
                if route:
                    up(route, 1)
                if project:
                    c = project
                    pe.wait_ge(qk_ready, c.count())
                    MM(mixed[:], ident16[:], mask16[:].rearrange("p j t -> p (j t)"), start=True, stop=False,
                       skip_group_check=True)
                    for j in range(J):
                        one = slice(j * T, (j + 1) * T)
                        last = MM(mixed[:, one], qt[:, one], kt[:, one], start=False, stop=True, skip_group_check=True)
                    last.then_inc(scores_done, 1)
                if project and project.fixed and project.n == 1:
                    pe.wait_ge(folded, 1)
                    for e in range(E):
                        MM(hidden[0][:, e:e + 1], w1_sb[0:C, e], beta_sb[:], start=True, stop=True)
                    MM(hidden[0][:, E:2 * E], beta_row[:], wr_sb[0:C], start=True, stop=True).then_inc(folded, 1)
                if route:
                    up(route, 2)
                    up(route, 3)
                if close:
                    c = close
                    pe.wait_ge(sum_step, c.count(3))
                    if project:
                        pe.wait_ge(v_ready, project.count())
                    for j in range(J):
                        last = nc.tensor.transpose(values[:, j * T:(j + 1) * T], y_sum[:, j * T:(j + 1) * T], ident[:])
                    last.then_inc(closed, 1)
                if route:
                    down(route, 0)
                    up(route, 4)
                if route:
                    up(route, 5)
                    down(route, 1)

            pe.wait_ge(consts, 6)
            pipeline(pe, TILES, step)


_INS = ["x", "L0_tok_blur_kernel", "L0_attn_Wq", "L0_attn_bq", "L0_attn_Wk", "L0_attn_bk", "L0_attn_Wv", "L0_attn_bv",
        "L0_ffn_gamma", "L0_ffn_beta", "L0_ffn_Wr", "L0_ffn_br", "L0_ffn_W1", "L0_ffn_b1", "L0_ffn_W2", "L0_ffn_b2"]


def kernel(**inputs):
    import numpy as np
    import concourse.bacc as bacc
    from concourse.bass_utils import run_bass_kernel_spmd

    nc = bacc.Bacc("TRN2", target_bir_lowering=False, num_devices=1)
    arrays, args = {}, []
    for name in _INS:
        a = np.ascontiguousarray(inputs[name])
        arrays[f"in_{name}"] = a
        args.append(nc.dram_tensor(f"in_{name}", a.shape, mybir.dt.from_np(a.dtype), kind="ExternalInput").ap())
    batch, time, channels = inputs["x"].shape
    out = nc.dram_tensor("out", (batch, time // 2, channels), F32, kind="ExternalOutput").ap()
    w_dram = nc.dram_tensor("w_dram", (2, 8 * 512), F32, kind="Internal").ap()
    audio_tower(nc, *args, out, w_dram)
    return run_bass_kernel_spmd(nc, [arrays], core_ids=[0]).results[0]["out"]
```
